# Optimizing a Trainium2 kernel written in Bass

```python
import numpy as np
import jax
import jax.numpy as jnp

def _softmax(x, axis=-1):
    return jax.nn.softmax(x, axis=axis)

def _gelu(x):
    return jax.nn.gelu(x, approximate=True)

def _silu(x):
    return jax.nn.silu(x)

def _sigmoid(x):
    return jax.nn.sigmoid(x)

def _layernorm(x, axis=-1, eps=1e-05):
    m = jnp.mean(x, axis=axis, keepdims=True)
    v = jnp.var(x, axis=axis, keepdims=True)
    return (x - m) / jnp.sqrt(v + eps)

def _scatter_add(tgt, idx, src, axis=0):
    return tgt.at[idx].add(src)

def _segment_sum(src, seg, n):
    return jax.ops.segment_sum(src, seg, n)
kernel_name = 'mk_adj_seq_d1_adj_r2_b36a2c'

def setup_inputs(seed: int=0):
    np.random.seed(seed)
    _w = jnp.asarray

    def _rec_inputs():
        import jax
        import jax.numpy as jnp
        _gk = jax.random.key(seed)
        x = -0.0005207 + 1.001 * jax.random.normal(jax.random.fold_in(_gk, 1), (64, 128, 256), jnp.float32)
        _a = jax.random.bernoulli(jax.random.fold_in(_gk, 2), 0.0625, (64, 128, 128))
        adj = _a
        return (x, adj)
    x, adj = _rec_inputs()

    def _L0_gnn_setup():
        import jax, jax.numpy as jnp
        import numpy as np
        HIDDEN = 256
        HEADS = 8
        HEAD_DIM = HIDDEN // HEADS
        D_FF = 4 * HIDDEN
        NEG = -1000000000.0

        def _layernorm(x, g, b, eps=1e-05):
            mu = jnp.mean(x, axis=-1, keepdims=True)
            var = jnp.var(x, axis=-1, keepdims=True)
            return (x - mu) * jax.lax.rsqrt(var + eps) * g + b
        key = jax.random.key(seed)
        ks = jax.random.split(key, 16)
        B, S = (2, 1024)
        s = 1.0 / np.sqrt(HIDDEN)
        inp = {'x': jax.random.normal(ks[0], (B, S, HIDDEN), dtype=jnp.float32), 'adj_mask': jax.random.bernoulli(ks[1], 0.5, (B, S, S)), 'ln1_g': jnp.ones((HIDDEN,), jnp.float32), 'ln1_b': jnp.zeros((HIDDEN,), jnp.float32), 'ln2_g': jnp.ones((HIDDEN,), jnp.float32), 'ln2_b': jnp.zeros((HIDDEN,), jnp.float32), 'Wq': jax.random.uniform(ks[2], (HIDDEN, HIDDEN), jnp.float32, -s, s), 'bq': jnp.zeros((HIDDEN,), jnp.float32), 'Wk': jax.random.uniform(ks[3], (HIDDEN, HIDDEN), jnp.float32, -s, s), 'bk': jnp.zeros((HIDDEN,), jnp.float32), 'Wv': jax.random.uniform(ks[4], (HIDDEN, HIDDEN), jnp.float32, -s, s), 'bv': jnp.zeros((HIDDEN,), jnp.float32), 'Wo': jax.random.uniform(ks[5], (HIDDEN, HIDDEN), jnp.float32, -s, s), 'bo': jnp.zeros((HIDDEN,), jnp.float32), 'W1': jax.random.uniform(ks[6], (HIDDEN, D_FF), jnp.float32, -s, s), 'b1': jnp.zeros((D_FF,), jnp.float32), 'W2': jax.random.uniform(ks[7], (D_FF, HIDDEN), jnp.float32, -1.0 / np.sqrt(D_FF), 1.0 / np.sqrt(D_FF)), 'b2': jnp.zeros((HIDDEN,), jnp.float32)}
        return inp
    _L0_gnn_all = _L0_gnn_setup()
    _L0_gnn_in = {k: v for k, v in _L0_gnn_all.items() if k in ('ln1_g', 'ln1_b', 'ln2_g', 'ln2_b', 'Wq', 'bq', 'Wk', 'bk', 'Wv', 'bv', 'Wo', 'bo', 'W1', 'b1', 'W2', 'b2')}
    del _L0_gnn_all
    return {'x': x, 'adj': adj, 'L0_gnn_ln1_g': _L0_gnn_in['ln1_g'], 'L0_gnn_ln1_b': _L0_gnn_in['ln1_b'], 'L0_gnn_ln2_g': _L0_gnn_in['ln2_g'], 'L0_gnn_ln2_b': _L0_gnn_in['ln2_b'], 'L0_gnn_Wq': _L0_gnn_in['Wq'], 'L0_gnn_bq': _L0_gnn_in['bq'], 'L0_gnn_Wk': _L0_gnn_in['Wk'], 'L0_gnn_bk': _L0_gnn_in['bk'], 'L0_gnn_Wv': _L0_gnn_in['Wv'], 'L0_gnn_bv': _L0_gnn_in['bv'], 'L0_gnn_Wo': _L0_gnn_in['Wo'], 'L0_gnn_bo': _L0_gnn_in['bo'], 'L0_gnn_W1': _L0_gnn_in['W1'], 'L0_gnn_b1': _L0_gnn_in['b1'], 'L0_gnn_W2': _L0_gnn_in['W2'], 'L0_gnn_b2': _L0_gnn_in['b2']}

def reference(x, adj, L0_gnn_ln1_g, L0_gnn_ln1_b, L0_gnn_ln2_g, L0_gnn_ln2_b, L0_gnn_Wq, L0_gnn_bq, L0_gnn_Wk, L0_gnn_bk, L0_gnn_Wv, L0_gnn_bv, L0_gnn_Wo, L0_gnn_bo, L0_gnn_W1, L0_gnn_b1, L0_gnn_W2, L0_gnn_b2):
    import jax
    import jax.numpy as jnp

    def _L0_gnn_ref(x, adj_mask, ln1_g, ln1_b, ln2_g, ln2_b, Wq, bq, Wk, bk, Wv, bv, Wo, bo, W1, b1, W2, b2):
        import jax, jax.numpy as jnp
        import numpy as np
        HIDDEN = 256
        HEADS = 8
        HEAD_DIM = HIDDEN // HEADS
        D_FF = 4 * HIDDEN
        NEG = -1000000000.0

        def _layernorm(x, g, b, eps=1e-05):
            mu = jnp.mean(x, axis=-1, keepdims=True)
            var = jnp.var(x, axis=-1, keepdims=True)
            return (x - mu) * jax.lax.rsqrt(var + eps) * g + b
        B, S, H = x.shape
        nx = _layernorm(x, ln1_g, ln1_b)
        q = (nx @ Wq + bq).reshape(B, S, HEADS, HEAD_DIM)
        k = (nx @ Wk + bk).reshape(B, S, HEADS, HEAD_DIM)
        v = (nx @ Wv + bv).reshape(B, S, HEADS, HEAD_DIM)
        scores = jnp.einsum('bqhd,bkhd->bhqk', q, k) / np.sqrt(HEAD_DIM)
        scores = jnp.where(adj_mask[:, None, :, :], scores, NEG)
        attn = jax.nn.softmax(scores, axis=-1)
        out = jnp.einsum('bhqk,bkhd->bqhd', attn, v).reshape(B, S, H)
        out = out @ Wo + bo
        x = x + out
        nx = _layernorm(x, ln2_g, ln2_b)
        mlp = jax.nn.gelu(nx @ W1 + b1, approximate=False) @ W2 + b2
        return x + mlp
    x = _L0_gnn_ref(x, adj, L0_gnn_ln1_g, L0_gnn_ln1_b, L0_gnn_ln2_g, L0_gnn_ln2_b, L0_gnn_Wq, L0_gnn_bq, L0_gnn_Wk, L0_gnn_bk, L0_gnn_Wv, L0_gnn_bv, L0_gnn_Wo, L0_gnn_bo, L0_gnn_W1, L0_gnn_b1, L0_gnn_W2, L0_gnn_b2)
    return x

_drawn_inputs = setup_inputs


def setup_inputs(seed=0):
    import zlib

    import numpy as np

    out = dict(_drawn_inputs(seed))
    spreads = {'L0_gnn_ln1_g': (1.0, 0.547),
     'L0_gnn_ln1_b': (0.0, 0.1),
     'L0_gnn_ln2_g': (1.0, 0.2),
     'L0_gnn_ln2_b': (0.0, 0.382),
     'L0_gnn_bq': (0.0, 0.8),
     'L0_gnn_bk': (0.0, 0.8),
     'L0_gnn_bv': (0.0, 0.1),
     'L0_gnn_bo': (0.0, 0.1),
     'L0_gnn_b1': (0.0, 0.1),
     'L0_gnn_b2': (0.0, 0.1)}
    factors = {}
    for name, (base, spread) in spreads.items():
        noise = np.random.default_rng([zlib.crc32(name.encode()), seed]).standard_normal(out[name].shape)
        drawn = base * np.exp(spread * noise) if base else spread * noise
        out[name] = jnp.asarray(drawn.astype(out[name].dtype))
    for name, factor in factors.items():
        out[name] = (out[name] * factor).astype(out[name].dtype)
    return out
```

```python
from contextlib import ExitStack

import concourse.bass as bass
from concourse import mybir

F32 = mybir.dt.float32
F32R = mybir.dt.float32r
I32 = mybir.dt.int32
U8 = mybir.dt.uint8
ALU = mybir.AluOpType
ACT = mybir.ActivationFunctionType

P = 128
G = 4
HEADS = 8
EPS = 1e-5
MASKED = 1e30
RSQRT_GUESS = 1597463007.0
NEWTON = 3
RS_STEPS = 5 + 3 * NEWTON
BANK_COLS = 512

TA, TB, WA, WB = 4, 5, 6, 7


def wait(eng, sem, value):
    if isinstance(value, int) and value <= 0:
        return
    eng.wait_ge(sem, value)


def hold_for(eng, sem, value, passed):
    if isinstance(value, int):
        return wait(eng, sem, value)
    eng.wait_ge(sem, value)
    eng.sem_inc(passed, 1)


def graph_layer(nc, x, adj, ln1_g, ln1_b, ln2_g, ln2_b, Wq, bq, Wk, bk, Wv, bv, Wo, bo, W1, b1, W2, b2, out):
    B, S, H = x.shape
    FF = W1.shape[1]
    NG = B // G
    D = H // HEADS
    KC = H // P
    FC = FF // P
    R = P // D
    TOK = G * P
    SCALE = float(D) ** -0.5
    assert S == P and D == 32 and TOK == BANK_COLS and KC == 2

    with ExitStack() as ctx:
        def sb(name, shape, dt=F32):
            return ctx.enter_context(nc.sbuf_tensor(name, shape, dt))

        def sem(name):
            return ctx.enter_context(nc.semaphore(name))

        ps = ctx.enter_context(nc.psum_tensor("ps", [P, 8, BANK_COLS], F32))

        w_hi = sb("w_hi", [P, 4, KC, H], F32R)
        w_lo = sb("w_lo", [P, 4, KC, H], F32R)
        w1_hi = sb("w1_hi", [P, KC, FF], F32R)
        w1_lo = sb("w1_lo", [P, KC, FF], F32R)
        w2_hi = sb("w2_hi", [P, FC, H], F32R)
        w2_lo = sb("w2_lo", [P, FC, H], F32R)
        stage_a = sb("stage_a", [P, 4, KC, H])
        stage_b = sb("stage_b", [P, KC, FF])
        stage_c = sb("stage_c", [P, FC, H])
        g1c, b1c, g2c, b2c = (sb(n, [P, KC]) for n in ("g1c", "b1c", "g2c", "b2c"))
        bqkv = sb("bqkv", [P, 3, KC])
        bff = sb("bff", [P, FC])
        qkv_bias = sb("qkv_bias", [P, 3, KC])
        ff_bias = sb("ff_bias", [P, FC])
        v_bias_wide = sb("v_bias_wide", [P, KC, P])
        bo_row = sb("bo_row", [P, H])
        b2_row = sb("b2_row", [P, H])
        o_bias_row = sb("o_bias_row", [P, H])
        ident = sb("ident", [P, P])

        x_in = sb("x_in", [P, G, H])
        adj_in = sb("adj_in", [P, G, S], U8)
        mask = sb("mask", [P, G, S])
        x_res = sb("x_res", [P, G, H])
        x_hat = sb("x_hat", [P, G, H])
        xT_hi = sb("xT_hi", [P, KC, TOK], F32R)
        xT_lo = sb("xT_lo", [P, KC, TOK], F32R)
        qT = sb("qT", [P, KC, TOK])
        kT = sb("kT", [P, KC, TOK])
        v_sb = sb("v_sb", [P, G, H])
        masked = sb("masked", [P, HEADS, S])
        row_max = sb("row_max", [P, HEADS])
        neg_max = sb("neg_max", [P, HEADS])
        prob = sb("prob", [P, HEADS, S])
        row_sum = sb("row_sum", [P, HEADS])
        inv_sum = sb("inv_sum", [P, HEADS])
        prob_n = sb("prob_n", [P, HEADS, S])
        pT = sb("pT", [P, HEADS, S])
        oT_hi = sb("oT_hi", [P, KC, P], F32R)
        oT_lo = sb("oT_lo", [P, KC, P], F32R)
        x2 = sb("x2", [P, G, H])
        x2_res = sb("x2_res", [P, G, H])
        x2_hat = sb("x2_hat", [P, G, H])
        x2T_hi = sb("x2T_hi", [P, KC, TOK], F32R)
        x2T_lo = sb("x2T_lo", [P, KC, TOK], F32R)
        h_f32 = sb("h_f32", [P, 2, TOK])
        h_hi = sb("h_hi", [P, FC, TOK], F32R)
        h_lo = sb("h_lo", [P, FC, TOK], F32R)
        y_out = sb("y_out", [P, G, H])
        st = [sb(f"st{n}", [P, G, 6]) for n in (1, 2)]
        mv = [sb(f"mv{n}", [P, G, 2]) for n in (1, 2)]
        neg_mu = [sb(f"neg_mu{n}", [P, G]) for n in (1, 2)]
        rstd = [sb(f"rstd{n}", [P, G]) for n in (1, 2)]
        var_eps = sb("var_eps", [P, G])
        neg_half = sb("neg_half", [P, G])
        nt = sb("nt", [P, G])
        half_bits = sb("half_bits", [P, G], I32)

        wa_in, wb_in, wc_in, vec_in = (sem(n) for n in ("wa_in", "wb_in", "wc_in", "vec_in"))
        x_loaded, adj_loaded, y_stored = (sem(n) for n in ("x_loaded", "adj_loaded", "y_stored"))
        ident_ready, bias_mm, bias_ready, wide_ready, orow_mm, orow_ready, w_ready, fold = (
            sem(n) for n in ("ident_ready", "bias_mm", "bias_ready", "wide_ready", "orow_mm", "orow_ready",
                             "w_ready", "fold"))
        pe_xT, pe_qk, pe_v, pe_score, pe_pT, pe_pv, pe_wo, pe_x2T, pe_w1, pe_w2 = (
            sem(n) for n in ("pe_xT", "pe_qk", "pe_v", "pe_score", "pe_pT", "pe_pv", "pe_wo", "pe_x2T",
                             "pe_w1", "pe_w2"))
        xT_hi_ok, qk_ok, exp_ok, x2T_hi_ok, h_f32_ok, h_hi_ok, pT_a_ok, oT_hi_ok = (
            sem(n) for n in ("xT_hi_ok", "qk_ok", "exp_ok", "x2T_hi_ok", "h_f32_ok", "h_hi_ok", "pT_a_ok",
                             "oT_hi_ok"))
        xT_lo_ok, v_ok, max_ok, neg_max_ok, inv_ok, x2T_lo_ok, h_lo_ok, pT_b_ok, oT_lo_ok, x2_ok, y_ok = (
            sem(n) for n in ("xT_lo_ok", "v_ok", "max_ok", "neg_max_ok", "inv_ok", "x2T_lo_ok", "h_lo_ok",
                             "pT_b_ok", "oT_lo_ok", "x2_ok", "y_ok"))
        stats_ok = [sem(f"stats{n}_ok") for n in (1, 2)]
        mv_ok = [sem(f"mv{n}_ok") for n in (1, 2)]
        rs_step = [sem(f"rs_step{n}") for n in (1, 2)]
        prob_n_ok, x_hat_ok, x_res_ok, x2_res_ok, x2_hat_ok, mask_ok = (
            sem(n) for n in ("prob_n_ok", "x_hat_ok", "x_res_ok", "x2_res_ok", "x2_hat_ok", "mask_ok"))

        pool_passed, dve_passed = sem("pool_passed"), sem("dve_passed")

        block = ctx.enter_context(nc.Block())

        @block.sync
        def _(sp):
            def load_group(i, first_graph):
                wait(sp, x_hat_ok, i * G)
                wait(sp, x_res_ok, i * G)
                wait(sp, mask_ok, i)
                sp.dma_start(x_in[:, :, :], x[bass.ds(first_graph, G)].rearrange("g p d -> p g d")).then_inc(x_loaded, 16)
                sp.dma_start(adj_in[:, :, :], adj[bass.ds(first_graph, G)].rearrange("g p d -> p g d")).then_inc(adj_loaded, 16)

            def store_group(m, first_graph):
                for j in range(G):
                    wait(sp, y_ok, 1 + m * G + (j + 1))
                    sp.dma_start(out[bass.ds(first_graph + j, 1)].rearrange("g p d -> p (g d)"),
                                 y_out[:, j, :]).then_inc(y_stored, 16)

            sp.sem_inc(y_stored, 1)
            sp.sem_inc(y_ok, 1)
            for n, w in enumerate((Wq, Wk, Wv, Wo)):
                sp.dma_start(stage_a[:, n, :, :], w.rearrange("(c p) n -> p c n", p=P)).then_inc(wa_in, 16)
            load_group(0, 0)
            sp.dma_start(stage_b[:, :, :], W1.rearrange("(c p) n -> p c n", p=P)).then_inc(wb_in, 16)
            sp.dma_start(stage_c[:, :, :], W2.rearrange("(c p) n -> p c n", p=P)).then_inc(wc_in, 16)
            load_group(1, G)
            with sp.Fori(1, NG - 1) as i:
                ahead = sp.snap(i * G + G)
                behind = [sp.snap(i * G - G + j) for j in range(G)]
                load_group(i + 1, ahead)
                for j in range(G):
                    sp.wait_ge(y_ok, 1 + i * G - G + (j + 1))
                    sp.dma_start(out[bass.ds(behind[j], 1)].rearrange("g p d -> p (g d)"),
                                 y_out[:, j, :]).then_inc(y_stored, 16)
            store_group(NG - 2, (NG - 2) * G)
            store_group(NG - 1, (NG - 1) * G)
            sp.wait_ge(y_stored, 1 + 16 * B)

        @block.tensor
        def _(pe):
            def split_mm(dst, pairs):
                passes = [p for sh, sl, mh, ml in pairs for p in ((sh, mh), (sh, ml), (sl, mh))]
                for n, (s, m) in enumerate(passes):
                    last = pe.matmul(dst, s, m, start=(n == 0), stop=(n == len(passes) - 1))
                return last

            def transpose_group(src, done):
                for c in range(KC):
                    for j in range(G):
                        last = pe.transpose(ps[:, TA + c, j * P:(j + 1) * P], src[:, j, c * P:(c + 1) * P], ident[:, :])
                    last.then_inc(done, 1)

            def qkv(i):
                wait(pe, x_hat_ok, i * G + G)
                transpose_group(x_hat, pe_xT)
                wait(pe, xT_hi_ok, i * KC + KC)
                wait(pe, xT_lo_ok, i * KC + KC)
                for n in range(2):
                    for c in range(KC):
                        cols = slice(c * P, (c + 1) * P)
                        split_mm(ps[:, n * KC + c, :],
                                 [(w_hi[:, n, k, cols], w_lo[:, n, k, cols], xT_hi[:, k, :], xT_lo[:, k, :])
                                  for k in range(KC)]).then_inc(pe_qk, 1)
                wait(pe, x2_ok, i * G)
                wait(pe, y_ok, 1 + i * G - G)
                for j, bank in enumerate((WA, WB, TA, TB)):
                    rows = slice(j * P, (j + 1) * P)
                    split_mm(ps[:, bank, 0:H],
                             [(xT_hi[:, k, rows], xT_lo[:, k, rows], w_hi[:, 2, k, :], w_lo[:, 2, k, :])
                              for k in range(KC)]).then_inc(pe_v, 1)

            def scores(i, j):
                if j == 0:
                    wait(pe, qk_ok, i * 4 + 4)
                rows = slice(j * P, (j + 1) * P)
                for c in range(KC):
                    for r in range(R):
                        part = slice(r * D, (r + 1) * D)
                        last = pe.matmul(ps[:, r, c * P:(c + 1) * P], qT[part, c, rows], kT[part, c, rows],
                                         start=True, stop=True)
                last.then_inc(pe_score, 1)

            def transpose_probs(i, j):
                if j == 0:
                    wait(pe, v_ok, i * G + G)
                else:
                    wait(pe, oT_hi_ok, i * G + j)
                    wait(pe, oT_lo_ok, i * G + j)
                for c in range(KC):
                    wait(pe, prob_n_ok, i * G * KC + (j * KC + c + 1))
                    for r in range(R):
                        last = pe.transpose(ps[:, TA + c, r * P:(r + 1) * P], prob_n[:, c * R + r, :], ident[:, :])
                    last.then_inc(pe_pT, 1)

            def attend(i, j):
                wait(pe, pT_a_ok, i * G + (j + 1))
                wait(pe, pT_b_ok, i * G + (j + 1))
                for c in range(KC):
                    for r in range(R):
                        h = c * R + r
                        last = pe.matmul(ps[r * D:(r + 1) * D, TA, c * P:(c + 1) * P], v_sb[:, j, h * D:(h + 1) * D],
                                         pT[:, h, :], start=True, stop=True)
                last.then_inc(pe_pv, 1)

            def project(i, j):
                wait(pe, oT_hi_ok, i * G + (j + 1))
                wait(pe, oT_lo_ok, i * G + (j + 1))
                wait(pe, x2_ok, i * G + j)
                split_mm(ps[:, WA, 0:H], [(oT_hi[:, k, :], oT_lo[:, k, :], w_hi[:, 3, k, :], w_lo[:, 3, k, :])
                                          for k in range(KC)]).then_inc(pe_wo, 1)

            def mlp_up(m):
                wait(pe, x2_hat_ok, m * G + G)
                wait(pe, v_ok, m * G + 2 * G if not last_mlp[0] else NG * G)
                transpose_group(x2_hat, pe_x2T)
                wait(pe, x2T_hi_ok, m * KC + KC)
                wait(pe, x2T_lo_ok, m * KC + KC)
                if last_mlp[0]:
                    wait(pe, x2_ok, NG * G)
                    wait(pe, y_ok, 1 + (NG - 1) * G)
                for f in range(FC):
                    cols = slice(f * P, (f + 1) * P)
                    if f >= 2:
                        wait(pe, h_hi_ok, m * FC + (f - 1))
                    split_mm(ps[:, WA + f % 2, :],
                             [(w1_hi[:, k, cols], w1_lo[:, k, cols], x2T_hi[:, k, :], x2T_lo[:, k, :])
                              for k in range(KC)]).then_inc(pe_w1, 1)

            def mlp_down(m, j, half=None):
                rows = slice(j * P, (j + 1) * P)
                passes = [p for f in range(FC) for p in ((h_hi[:, f, rows], w2_hi[:, f, :]),
                                                         (h_hi[:, f, rows], w2_lo[:, f, :]),
                                                         (h_lo[:, f, rows], w2_hi[:, f, :]))]
                first, end = {None: (0, 3 * FC), 0: (0, 3 * FC // 2), 1: (3 * FC // 2, 3 * FC)}[half]
                if first == 0:
                    wait(pe, h_hi_ok, m * FC + FC)
                    wait(pe, h_lo_ok, m * FC + FC)
                    wait(pe, y_ok, 1 + m * G + j)
                for n in range(first, end):
                    last = pe.matmul(ps[:, WB, 0:H], *passes[n], start=(n == 0), stop=(n == 3 * FC - 1))
                if end == 3 * FC:
                    last.then_inc(pe_w2, 1)

            last_mlp = [False]

            def body(i, with_mlp):
                m = i - 1
                down = (lambda j, half=None: mlp_down(m, j, half)) if with_mlp else (lambda j, half=None: None)
                qkv(i)
                scores(i, 0)
                if with_mlp:
                    mlp_up(m)
                transpose_probs(i, 0)
                scores(i, 1)
                attend(i, 0)
                down(0)
                transpose_probs(i, 1)
                scores(i, 2)
                project(i, 0)
                attend(i, 1)
                down(1)
                transpose_probs(i, 2)
                scores(i, 3)
                project(i, 1)
                attend(i, 2)
                down(2)
                transpose_probs(i, 3)
                project(i, 2)
                down(3, 0)
                attend(i, 3)
                down(3, 1)
                project(i, 3)

            pe.wait_ge(wa_in, 64)
            pe.wait_ge(vec_in, 16 * 10)
            for n in range(3):
                for c in range(KC):
                    for k in range(KC):
                        pe.matmul(ps[:, 0, n * KC + c:n * KC + c + 1], stage_a[:, n, k, c * P:(c + 1) * P],
                                  b1c[:, k:k + 1], start=(k == 0), stop=(k == KC - 1))
            pe.wait_ge(wb_in, 16)
            for f in range(FC):
                for k in range(KC):
                    last = pe.matmul(ps[:, 0, 8 + f:9 + f], stage_b[:, k, f * P:(f + 1) * P], b2c[:, k:k + 1],
                                     start=(k == 0), stop=(k == KC - 1))
            last.then_inc(bias_mm, 1)
            pe.wait_ge(wide_ready, 1)
            for k in range(KC):
                last = pe.matmul(ps[:, 1, 0:H], v_bias_wide[:, k, :], stage_a[:, 3, k, :], start=(k == 0), stop=(k == KC - 1))
            last.then_inc(orow_mm, 1)
            pe.wait_ge(ident_ready, 2)
            pe.wait_ge(orow_ready, 1)
            pe.wait_ge(w_ready, 12)
            body(0, False)
            with pe.Fori(1, NG) as i:
                body(i, True)
            last_mlp[0] = True
            mlp_up(NG - 1)
            for j in range(G):
                mlp_down(NG - 1, j)

        @block.scalar
        def _(act):
            def copy_T(i, hi, mm_done, done):
                for c in range(KC):
                    wait(act, mm_done, i * KC + (c + 1))
                    act.copy(hi[:, c, :], ps[:, TA + c, :]).then_inc(done, 1)

            def q_k(i):
                for n, dst in enumerate((qT, kT)):
                    for c in range(KC):
                        wait(act, pe_qk, i * 4 + (n * KC + c + 1))
                        act.activation(dst[:, c, :], ps[:, n * KC + c, :], ACT.Identity, bias=qkv_bias[:, n, c:c + 1],
                                       scale=(SCALE, 1.0)[n]).then_inc(qk_ok, 1)

            def exps(i, j):
                for c in range(KC):
                    wait(act, neg_max_ok, i * G * KC + (j * KC + c + 1))
                    for h in range(c * R, (c + 1) * R):
                        last = act.activation(prob[:, h, :], masked[:, h, :], ACT.Exp, bias=neg_max[:, h:h + 1],
                                              accum_out=row_sum[:, h:h + 1])
                    last.then_inc(exp_ok, 1)

            def probs_T(i, j):
                wait(act, pe_pT, i * G * KC + (j * KC + 1))
                act.copy(pT[:, 0:R, :], ps[:, TA, :].rearrange("p (h q) -> p h q", h=R)).then_inc(pT_a_ok, 1)

            def attn_hi(i, j):
                wait(act, pe_pv, i * G + (j + 1))
                act.copy(oT_hi[:, :, :], ps[:, TA, 0:KC * P].rearrange("p (c q) -> p c q", c=KC)).then_inc(oT_hi_ok, 1)

            def gelus(m):
                copy_T(m, x2T_hi, pe_x2T, x2T_hi_ok)
                for f in range(FC):
                    wait(act, pe_w1, m * FC + (f + 1))
                    if f >= 2:
                        wait(act, h_lo_ok, m * FC + (f - 1))
                    act.activation(h_f32[:, f % 2, :], ps[:, WA + f % 2, :], ACT.Gelu,
                                   bias=ff_bias[:, f:f + 1]).then_inc(h_f32_ok, 1)
                    act.activation(h_hi[:, f, :], ps[:, WA + f % 2, :], ACT.Gelu,
                                   bias=ff_bias[:, f:f + 1]).then_inc(h_hi_ok, 1)

            def body(i, with_mlp):
                copy_T(i, xT_hi, pe_xT, xT_hi_ok)
                q_k(i)
                exps(i, 0)
                if with_mlp:
                    gelus(i - 1)
                for j in range(G):
                    probs_T(i, j)
                    if j + 1 < G:
                        exps(i, j + 1)
                    attn_hi(i, j)

            for t, src in ((g1c[:, :], ln1_g), (b1c[:, :], ln1_b), (g2c[:, :], ln2_g), (b2c[:, :], ln2_b), (bqkv[:, 0, :], bq),
                           (bqkv[:, 1, :], bk), (bqkv[:, 2, :], bv), (bff[:, :], b1)):
                act.dma_start(t, src.rearrange("(c p) -> p c", p=P), allow_slow_non_contiguous=True).then_inc(vec_in, 16)
            act.dma_start(bo_row[:, :], bo.partition_broadcast(P)).then_inc(vec_in, 16)
            act.dma_start(b2_row[:, :], b2.partition_broadcast(P)).then_inc(vec_in, 16)
            act.wait_ge(bias_ready, 3)
            body(0, False)
            with act.Fori(1, NG) as i:
                body(i, True)
            gelus(NG - 1)

        @block.vector
        def _(dve):
            def stats(ln, i, j, src):
                dve.bn_stats(st[ln][:, j, :], src[:, j, :]).then_inc(stats_ok[ln], 1)
                hold_for(dve, stats_ok[ln], i * G + (j + 1), dve_passed)
                dve.bn_aggr(mv[ln][:, j, :], st[ln][:, j, :]).then_inc(mv_ok[ln], 1)

            def rsqrt_var(ln, i):
                wait(dve, mv_ok[ln], i * G + G)
                step = [0]

                def link(ins):
                    step[0] += 1
                    ins.then_inc(rs_step[ln], 1)
                    wait(dve, rs_step[ln], i * RS_STEPS + step[0])

                y = rstd[ln]
                dve.tensor_scalar(neg_mu[ln][:, :], mv[ln][:, :, 0], -1.0, None, ALU.mult).then_inc(rs_step[ln], 1)
                step[0] += 1
                link(dve.tensor_scalar(var_eps[:, :], mv[ln][:, :, 1], EPS, None, ALU.add))
                link(dve.tensor_scalar(half_bits[:, :], var_eps[:, :].bitcast(I32), 1, None, ALU.logical_shift_right))
                link(dve.tensor_scalar(y[:, :].bitcast(I32), half_bits[:, :], -1.0, RSQRT_GUESS, ALU.mult, ALU.add))
                link(dve.tensor_scalar(neg_half[:, :], var_eps[:, :], -0.5, None, ALU.mult))
                for _ in range(NEWTON):
                    link(dve.tensor_tensor(nt[:, :], y[:, :], y[:, :], ALU.mult))
                    link(dve.tensor_tensor(var_eps[:, :], nt[:, :], neg_half[:, :], ALU.mult))
                    link(dve.scalar_tensor_tensor(out=y[:, :], in0=var_eps[:, :], scalar=1.5, in1=y[:, :],
                                                  op0=ALU.add, op1=ALU.mult))
                assert step[0] == RS_STEPS

            def lo_T(i, lo, hi, hi_ok, done):
                for c in range(KC):
                    wait(dve, hi_ok, i * KC + (c + 1))
                    dve.tensor_tensor(lo[:, c, :], ps[:, TA + c, :], hi[:, c, :], ALU.subtract).then_inc(done, 1)

            def values(i):
                for j, bank in enumerate((WA, WB, TA, TB)):
                    wait(dve, pe_v, i * G + (j + 1))
                    dve.tensor_copy(v_sb[:, j, :], ps[:, bank, 0:H]).then_inc(v_ok, 1)

            def maxima(i, j):
                if j == 0:
                    wait(dve, mask_ok, i + 1)
                hold_for(dve, pe_score, i * G + (j + 1), dve_passed)
                for c in range(KC):
                    for r in range(R):
                        h = c * R + r
                        last = dve.tensor_tensor_reduce(masked[:, h, :], ps[:, r, c * P:(c + 1) * P], mask[:, j, :],
                                                        1.0, -3.0e38, ALU.add, ALU.max, row_max[:, h:h + 1])
                    last.then_inc(max_ok, 1)
                    wait(dve, max_ok, i * G * KC + (j * KC + c + 1))
                    dve.tensor_scalar(neg_max[:, c * R:(c + 1) * R], row_max[:, c * R:(c + 1) * R], -1.0, None,
                                      ALU.mult).then_inc(neg_max_ok, 1)

            def inverse(i, j):
                wait(dve, exp_ok, i * G * KC + (j * KC + KC))
                dve.reciprocal(inv_sum[:, :], row_sum[:, :]).then_inc(inv_ok, 1)

            def probs_T(i, j):
                wait(dve, pe_pT, i * G * KC + (j * KC + KC))
                dve.tensor_copy(pT[:, R:2 * R, :], ps[:, TB, :].rearrange("p (h q) -> p h q", h=R)).then_inc(pT_b_ok, 1)

            def attn_lo(i, j):
                wait(dve, oT_hi_ok, i * G + (j + 1))
                dve.tensor_tensor(oT_lo[:, :, :], ps[:, TA, 0:KC * P].rearrange("p (c q) -> p c q", c=KC),
                                  oT_hi[:, :, :], ALU.subtract).then_inc(oT_lo_ok, 1)

            def residual(i, j):
                wait(dve, pe_wo, i * G + (j + 1))
                if j == 0:
                    wait(dve, x_res_ok, i * G + G)
                    wait(dve, x2_hat_ok, i * G)
                    wait(dve, x2_res_ok, i * G)
                dve.tensor_tensor(x2[:, j, :], ps[:, WA, 0:H], x_res[:, j, :], ALU.add).then_inc(x2_ok, 1)
                wait(dve, x2_ok, i * G + (j + 1))
                stats(1, i, j, x2)

            def gelu_lo(m):
                lo_T(m, x2T_lo, x2T_hi, x2T_hi_ok, x2T_lo_ok)
                for f in range(FC):
                    wait(dve, h_hi_ok, m * FC + (f + 1))
                    dve.tensor_tensor(h_lo[:, f, :], h_f32[:, f % 2, :], h_hi[:, f, :], ALU.subtract).then_inc(h_lo_ok, 1)

            def finish(m, j):
                wait(dve, pe_w2, m * G + (j + 1))
                wait(dve, x2_res_ok, m * G + (j + 1))
                wait(dve, y_stored, 1 + m * G * 16)
                dve.tensor_tensor(y_out[:, j, :], ps[:, WB, 0:H], x2_res[:, j, :], ALU.add).then_inc(y_ok, 1)

            def ln1_stats(i, j):
                if j == 0:
                    wait(dve, x_loaded, (i + 1) * 16)
                    wait(dve, x_hat_ok, i * G)
                stats(0, i, j, x_in)

            def body(i, with_mlp, with_next):
                m = i - 1
                lo_T(i, xT_lo, xT_hi, xT_hi_ok, xT_lo_ok)
                values(i)
                maxima(i, 0)
                inverse(i, 0)
                if with_mlp:
                    gelu_lo(m)
                for j in range(G):
                    probs_T(i, j)
                    if j + 1 < G:
                        maxima(i, j + 1)
                    attn_lo(i, j)
                    if j + 1 < G:
                        inverse(i, j + 1)
                    if j >= 1:
                        residual(i, j - 1)
                    if with_mlp:
                        finish(m, j)
                    if with_next and j < 2:
                        ln1_stats(i + 1, 2 * j)
                        ln1_stats(i + 1, 2 * j + 1)
                    if with_next and j == 2:
                        rsqrt_var(0, i + 1)
                residual(i, G - 1)
                rsqrt_var(1, i)

            for j in range(G):
                ln1_stats(0, j)
            rsqrt_var(0, 0)
            dve.wait_ge(wa_in, 64)
            dve.wait_ge(vec_in, 16 * 10)
            for n in range(3):
                for k in range(KC):
                    dve.tensor_scalar(w_hi[:, n, k, :], stage_a[:, n, k, :], g1c[:, k:k + 1], None, ALU.mult).then_inc(fold, 1)
            dve.tensor_copy(w_hi[:, 3, :, :], stage_a[:, 3, :, :]).then_inc(fold, 1)
            dve.wait_ge(fold, 7)
            for n in range(3):
                for k in range(KC):
                    dve.scalar_tensor_tensor(out=w_lo[:, n, k, :], in0=stage_a[:, n, k, :], scalar=g1c[:, k:k + 1],
                                             in1=w_hi[:, n, k, :], op0=ALU.mult, op1=ALU.subtract).then_inc(w_ready, 1)
            dve.tensor_tensor(w_lo[:, 3, :, :], stage_a[:, 3, :, :], w_hi[:, 3, :, :], ALU.subtract).then_inc(w_ready, 1)
            dve.wait_ge(bias_mm, 1)
            dve.tensor_tensor(qkv_bias[:, :, :], ps[:, 0, 0:3 * KC].rearrange("p (n c) -> p n c", n=3), bqkv[:, :, :],
                              ALU.add).then_inc(bias_ready, 1)
            dve.tensor_tensor(ff_bias[:, :], ps[:, 0, 8:8 + FC], bff[:, :], ALU.add).then_inc(bias_ready, 1)
            dve.wait_ge(bias_ready, 2)
            dve.tensor_scalar(qkv_bias[:, 0, :], qkv_bias[:, 0, :], SCALE, None, ALU.mult).then_inc(bias_ready, 1)
            dve.tensor_copy(v_bias_wide[:, :, :], qkv_bias[:, 2, :].unsqueeze(2).broadcast_to([P, KC, P])).then_inc(wide_ready, 1)
            dve.wait_ge(orow_mm, 1)
            dve.tensor_tensor(o_bias_row[:, :], ps[:, 1, 0:H], bo_row[:, :], ALU.add).then_inc(orow_ready, 1)
            dve.wait_ge(wb_in, 16)
            for k in range(KC):
                dve.tensor_scalar(w1_hi[:, k, :], stage_b[:, k, :], g2c[:, k:k + 1], None, ALU.mult).then_inc(fold, 1)
            dve.wait_ge(wc_in, 16)
            for k in range(2):
                half = slice(k * FC // 2, (k + 1) * FC // 2)
                dve.tensor_copy(w2_hi[:, half, :], stage_c[:, half, :]).then_inc(fold, 1)
            dve.wait_ge(fold, 11)
            for k in range(KC):
                dve.scalar_tensor_tensor(out=w1_lo[:, k, :], in0=stage_b[:, k, :], scalar=g2c[:, k:k + 1],
                                         in1=w1_hi[:, k, :], op0=ALU.mult, op1=ALU.subtract).then_inc(w_ready, 1)
            for k in range(2):
                half = slice(k * FC // 2, (k + 1) * FC // 2)
                dve.tensor_tensor(w2_lo[:, half, :], stage_c[:, half, :], w2_hi[:, half, :], ALU.subtract).then_inc(w_ready, 1)
            dve.engine_nop().then_inc(w_ready, 1)
            body(0, False, True)
            with dve.Fori(1, NG - 1) as i:
                body(i, True, True)
            body(NG - 1, True, False)
            gelu_lo(NG - 1)
            for j in range(G):
                finish(NG - 1, j)

        @block.gpsimd
        def _(pool):
            def hold(sem, value):
                hold_for(pool, sem, value, pool_passed)

            def make_mask(i):
                hold(adj_loaded, (i + 1) * 16)
                hold(max_ok, i * G * KC)
                nc.gpsimd.tensor_scalar(mask[:, :, :], adj_in[:, :, :], MASKED, -MASKED, ALU.mult, ALU.add).then_inc(mask_ok, 1)

            def apply_ln(ln, i, dst, src, done):
                hold(rs_step[ln], (i + 1) * RS_STEPS)
                for j in range(G):
                    nc.gpsimd.tensor_scalar(dst[:, j, :], src[:, j, :], neg_mu[ln][:, j:j + 1], rstd[ln][:, j:j + 1],
                                            ALU.add, ALU.mult).then_inc(done, 1)

            def ln1(i):
                hold(pe_xT, i * KC)
                apply_ln(0, i, x_hat, x_in, x_hat_ok)

            def add_o_bias(i, j):
                wait(pool, x2_ok, i * G + (j - G + 1))
                nc.gpsimd.tensor_tensor(x_res[:, j, :], x_in[:, j, :], o_bias_row[:, :], ALU.add).then_inc(x_res_ok, 1)

            def normalise(i, j):
                wait(pool, inv_ok, i * G + (j + 1))
                for c in range(KC):
                    hs = slice(c * R, (c + 1) * R)
                    nc.gpsimd.tensor_tensor(prob_n[:, hs, :], prob[:, hs, :],
                                            inv_sum[:, hs].unsqueeze(2).broadcast_to([P, R, S]), ALU.mult).then_inc(prob_n_ok, 1)

            def add_b2(i, j):
                wait(pool, x2_ok, i * G + (j + 1))
                wait(pool, y_ok, 1 + i * G + (j - G + 1))
                nc.gpsimd.tensor_tensor(x2_res[:, j, :], x2[:, j, :], b2_row[:, :], ALU.add).then_inc(x2_res_ok, 1)

            def body(i, with_next):
                for j in range(G):
                    normalise(i, j)
                    if j >= 2:
                        add_b2(i, j - 2)
                        if with_next:
                            add_o_bias(i + 1, j - 2)
                if with_next:
                    ln1(i + 1)
                    make_mask(i + 1)
                for j in (G - 2, G - 1):
                    add_b2(i, j)
                    if with_next:
                        add_o_bias(i + 1, j)
                hold(pe_x2T, i * KC)
                apply_ln(1, i, x2_hat, x2, x2_hat_ok)

            nc.gpsimd.memset(ident[:, :], 0.0).then_inc(ident_ready, 1)
            pool.wait_ge(ident_ready, 1)
            nc.gpsimd.affine_select(out=ident[:, :], in_=ident[:, :], compare_op=ALU.not_equal, fill=1.0, base=0,
                                    pattern=[[-1, P]], channel_multiplier=1).then_inc(ident_ready, 1)
            ln1(0)
            make_mask(0)
            pool.wait_ge(orow_ready, 1)
            for j in range(G):
                add_o_bias(0, j)
            body(0, True)
            with pool.Fori(1, NG - 1) as i:
                body(i, True)
            body(NG - 1, False)


_INS = ["x", "adj"] + ["L0_gnn_" + n for n in ("ln1_g", "ln1_b", "ln2_g", "ln2_b", "Wq", "bq", "Wk", "bk", "Wv", "bv",
                                               "Wo", "bo", "W1", "b1", "W2", "b2")]


def kernel(**inputs):
    import numpy as _np
    import concourse.bacc as _bacc
    from concourse import mybir as _mybir
    from concourse.bass_utils import run_bass_kernel_spmd as _run

    nc = _bacc.Bacc("TRN2", target_bir_lowering=False, num_devices=1)
    arrays, args = {}, []
    for name in _INS:
        a = _np.ascontiguousarray(inputs[name])
        arrays[f"in_{name}"] = a
        args.append(nc.dram_tensor(f"in_{name}", a.shape, _mybir.dt.from_np(a.dtype), kind="ExternalInput").ap())
    out = nc.dram_tensor("out_0", arrays["in_x"].shape, _mybir.dt.float32, kind="ExternalOutput").ap()
    graph_layer(nc, *args, out)
    r = _run(nc, [arrays], core_ids=[0])
    return r.results[0]["out_0"]
```

```python
from contextlib import ExitStack

import concourse.bass as bass
from concourse import mybir

F32 = mybir.dt.float32
F32R = mybir.dt.float32r
I32 = mybir.dt.int32
U8 = mybir.dt.uint8
ALU = mybir.AluOpType
ACT = mybir.ActivationFunctionType

P = 128
G = 4
HEADS = 8
EPS = 1e-5
MASKED = 1e30
RSQRT_GUESS = 1597463007.0
NEWTON = 3
RS_PARTS = 1 + NEWTON
RS_STEPS = 5 + 3 * NEWTON
BANK_COLS = 512

TA, TB, WA, WB = 4, 5, 6, 7
UP_BANKS = (WA, WB, TA, TB)


def wait(eng, sem, value):
    if isinstance(value, int) and value <= 0:
        return
    eng.wait_ge(sem, value)


def hold_for(eng, sem, value, passed):
    if isinstance(value, int):
        return wait(eng, sem, value)
    eng.wait_ge(sem, value)
    eng.sem_inc(passed, 1)


def graph_layer(nc, x, adj, ln1_g, ln1_b, ln2_g, ln2_b, Wq, bq, Wk, bk, Wv, bv, Wo, bo, W1, b1, W2, b2, out):
    B, S, H = x.shape
    FF = W1.shape[1]
    NG = B // G
    D = H // HEADS
    KC = H // P
    FC = FF // P
    R = P // D
    TOK = G * P
    SCALE = float(D) ** -0.5
    assert S == P and D == 32 and TOK == BANK_COLS and KC == 2

    with ExitStack() as ctx:
        def sb(name, shape, dt=F32):
            return ctx.enter_context(nc.sbuf_tensor(name, shape, dt))

        def sem(name):
            return ctx.enter_context(nc.semaphore(name))

        ps = ctx.enter_context(nc.psum_tensor("ps", [P, 8, BANK_COLS], F32))

        w_hi = sb("w_hi", [P, 4, KC, H], F32R)
        w_lo = sb("w_lo", [P, 4, KC, H], F32R)
        w1_hi = sb("w1_hi", [P, KC, FF], F32R)
        w1_lo = sb("w1_lo", [P, KC, FF], F32R)
        w2_hi = sb("w2_hi", [P, FC, H], F32R)
        w2_lo = sb("w2_lo", [P, FC, H], F32R)
        stage_a = sb("stage_a", [P, 4, KC, H])
        stage_b = sb("stage_b", [P, KC, FF])
        stage_c = sb("stage_c", [P, FC, H])
        g1c, b1c, g2c, b2c = (sb(n, [P, KC]) for n in ("g1c", "b1c", "g2c", "b2c"))
        bqkv = sb("bqkv", [P, 3, KC])
        bff = sb("bff", [P, FC])
        qkv_bias = sb("qkv_bias", [P, 3, KC])
        ff_bias = sb("ff_bias", [P, FC])
        v_bias_wide = sb("v_bias_wide", [P, KC, P])
        bo_row = sb("bo_row", [P, H])
        b2_row = sb("b2_row", [P, H])
        o_bias_row = sb("o_bias_row", [P, H])
        ident = sb("ident", [P, P])

        x_in = sb("x_in", [P, G, H])
        adj_in = sb("adj_in", [P, G, S], U8)
        mask = sb("mask", [P, G, S])
        x_res = sb("x_res", [P, G, H])
        x_hat = sb("x_hat", [P, G, H])
        xT_hi = sb("xT_hi", [P, KC, TOK], F32R)
        xT_lo = sb("xT_lo", [P, KC, TOK], F32R)
        qT = sb("qT", [P, KC, TOK])
        kT = sb("kT", [P, KC, TOK])
        v_sb = sb("v_sb", [P, G, H])
        masked = sb("masked", [P, 2, HEADS, S])
        row_max = sb("row_max", [P, 2, HEADS])
        neg_max = sb("neg_max", [P, 2, HEADS])
        prob = sb("prob", [P, 2, HEADS, S])
        row_sum = sb("row_sum", [P, 2, HEADS])
        inv_sum = sb("inv_sum", [P, 2, HEADS])
        prob_n = sb("prob_n", [P, 2, HEADS, S])
        pT = sb("pT", [P, HEADS, S])
        oT_hi = sb("oT_hi", [P, KC, P], F32R)
        oT_lo = sb("oT_lo", [P, KC, P], F32R)
        x2 = sb("x2", [P, G, H])
        x2_res = sb("x2_res", [P, G, H])
        x2_hat = sb("x2_hat", [P, G, H])
        x2T_hi = sb("x2T_hi", [P, KC, TOK], F32R)
        x2T_lo = sb("x2T_lo", [P, KC, TOK], F32R)
        h_f32 = sb("h_f32", [P, 2, TOK])
        h_hi = sb("h_hi", [P, FC, TOK], F32R)
        h_lo = sb("h_lo", [P, FC, TOK], F32R)
        y_out = sb("y_out", [P, G, H])
        st = [sb(f"st{n}", [P, G, 6]) for n in (1, 2)]
        mv = [sb(f"mv{n}", [P, G, 2]) for n in (1, 2)]
        neg_mu = [sb(f"neg_mu{n}", [P, G]) for n in (1, 2)]
        rstd = [sb(f"rstd{n}", [P, G]) for n in (1, 2)]
        rs_tmp = [[sb(f"rs_{t}{n}", [P, G]) for t in ("var_eps", "neg_half", "a")] for n in (1, 2)]
        half_bits = sb("half_bits", [P, G], I32)

        wa_in, wb_in, wc_in, vec_in = (sem(n) for n in ("wa_in", "wb_in", "wc_in", "vec_in"))
        x_loaded, adj_loaded, y_stored = (sem(n) for n in ("x_loaded", "adj_loaded", "y_stored"))
        ident_ready, bias_mm, bias_ready, wide_ready, orow_mm, orow_ready, w_ready, fold = (
            sem(n) for n in ("ident_ready", "bias_mm", "bias_ready", "wide_ready", "orow_mm", "orow_ready",
                             "w_ready", "fold"))
        pe_xT, pe_qk, pe_v, pe_score, pe_pT, pe_pv, pe_wo, pe_x2T, pe_w1, pe_w2 = (
            sem(n) for n in ("pe_xT", "pe_qk", "pe_v", "pe_score", "pe_pT", "pe_pv", "pe_wo", "pe_x2T",
                             "pe_w1", "pe_w2"))
        xT_hi_ok, qk_ok, exp_ok, x2T_hi_ok, h_f32_ok, h_hi_ok, pT_a_ok, oT_hi_ok = (
            sem(n) for n in ("xT_hi_ok", "qk_ok", "exp_ok", "x2T_hi_ok", "h_f32_ok", "h_hi_ok", "pT_a_ok",
                             "oT_hi_ok"))
        xT_lo_ok, v_ok, max_ok, neg_max_ok, inv_ok, x2T_lo_ok, h_lo_ok, pT_b_ok, oT_lo_ok, x2_ok, y_ok = (
            sem(n) for n in ("xT_lo_ok", "v_ok", "max_ok", "neg_max_ok", "inv_ok", "x2T_lo_ok", "h_lo_ok",
                             "pT_b_ok", "oT_lo_ok", "x2_ok", "y_ok"))
        stats_ok = [sem(f"stats{n}_ok") for n in (1, 2)]
        mv_ok = [sem(f"mv{n}_ok") for n in (1, 2)]
        rs_step = [sem(f"rs_step{n}") for n in (1, 2)]
        prob_n_ok, x_hat_ok, x_res_ok, x2_res_ok, x2_hat_ok, mask_ok = (
            sem(n) for n in ("prob_n_ok", "x_hat_ok", "x_res_ok", "x2_res_ok", "x2_hat_ok", "mask_ok"))

        pool_passed, dve_passed = sem("pool_passed"), sem("dve_passed")

        block = ctx.enter_context(nc.Block())

        @block.sync
        def _(sp):
            def load_group(i, first_graph):
                wait(sp, x_hat_ok, i * G)
                wait(sp, x_res_ok, i * G)
                wait(sp, mask_ok, i)
                sp.dma_start(x_in[:, :, :], x[bass.ds(first_graph, G)].rearrange("g p d -> p g d")).then_inc(x_loaded, 16)
                sp.dma_start(adj_in[:, :, :], adj[bass.ds(first_graph, G)].rearrange("g p d -> p g d")).then_inc(adj_loaded, 16)

            def store_group(m, first_graph):
                for j in range(G):
                    wait(sp, y_ok, 1 + m * G + (j + 1))
                    sp.dma_start(out[bass.ds(first_graph + j, 1)].rearrange("g p d -> p (g d)"),
                                 y_out[:, j, :]).then_inc(y_stored, 16)

            sp.sem_inc(y_stored, 1)
            sp.sem_inc(y_ok, 1)
            for n, w in enumerate((Wq, Wk, Wv, Wo)):
                sp.dma_start(stage_a[:, n, :, :], w.rearrange("(c p) n -> p c n", p=P)).then_inc(wa_in, 16)
            load_group(0, 0)
            sp.dma_start(stage_b[:, :, :], W1.rearrange("(c p) n -> p c n", p=P)).then_inc(wb_in, 16)
            sp.dma_start(stage_c[:, :, :], W2.rearrange("(c p) n -> p c n", p=P)).then_inc(wc_in, 16)
            load_group(1, G)
            with sp.Fori(1, NG - 1) as i:
                ahead = sp.snap(i * G + G)
                behind = [sp.snap(i * G - G + j) for j in range(G)]
                load_group(i + 1, ahead)
                for j in range(G):
                    sp.wait_ge(y_ok, 1 + i * G - G + (j + 1))
                    sp.dma_start(out[bass.ds(behind[j], 1)].rearrange("g p d -> p (g d)"),
                                 y_out[:, j, :]).then_inc(y_stored, 16)
            store_group(NG - 2, (NG - 2) * G)
            store_group(NG - 1, (NG - 1) * G)
            sp.wait_ge(y_stored, 1 + 16 * B)

        @block.tensor
        def _(pe):
            def split_mm(dst, pairs):
                passes = [p for sh, sl, mh, ml in pairs for p in ((sh, mh), (sh, ml), (sl, mh))]
                for n, (s, m) in enumerate(passes):
                    last = pe.matmul(dst, s, m, start=(n == 0), stop=(n == len(passes) - 1))
                return last

            def transpose_group(src, done):
                for c in range(KC):
                    for j in range(G):
                        last = pe.transpose(ps[:, TA + c, j * P:(j + 1) * P], src[:, j, c * P:(c + 1) * P], ident[:, :])
                    last.then_inc(done, 1)

            def q_k(i):
                wait(pe, x_hat_ok, i * G + G)
                transpose_group(x_hat, pe_xT)
                wait(pe, xT_hi_ok, i * KC + KC)
                wait(pe, xT_lo_ok, i * KC + KC)
                for n in range(2):
                    for c in range(KC):
                        cols = slice(c * P, (c + 1) * P)
                        split_mm(ps[:, n * KC + c, :],
                                 [(w_hi[:, n, k, cols], w_lo[:, n, k, cols], xT_hi[:, k, :], xT_lo[:, k, :])
                                  for k in range(KC)]).then_inc(pe_qk, 1)

            def values(i):
                wait(pe, x2_ok, i * G)
                wait(pe, y_ok, 1 + i * G - G)
                for j, bank in enumerate((WA, WB, TA, TB)):
                    if j == 2 and not isinstance(i, int):
                        wait(pe, x2T_hi_ok, i * KC)
                        wait(pe, x2T_lo_ok, i * KC)
                    rows = slice(j * P, (j + 1) * P)
                    split_mm(ps[:, bank, 0:H],
                             [(xT_hi[:, k, rows], xT_lo[:, k, rows], w_hi[:, 2, k, :], w_lo[:, 2, k, :])
                              for k in range(KC)]).then_inc(pe_v, 1)

            def scores(i, j):
                if j == 0:
                    wait(pe, qk_ok, i * 4 + 4)
                else:
                    wait(pe, max_ok, i * G * KC + j * KC)
                rows = slice(j * P, (j + 1) * P)
                for c in range(KC):
                    for r in range(R):
                        part = slice(r * D, (r + 1) * D)
                        last = pe.matmul(ps[:, r, c * P:(c + 1) * P], qT[part, c, rows], kT[part, c, rows],
                                         start=True, stop=True)
                last.then_inc(pe_score, 1)

            def transpose_probs(i, j):
                if j == 0:
                    wait(pe, v_ok, i * G + G)
                    if not isinstance(i, int):
                        wait(pe, h_hi_ok, i * FC)
                else:
                    wait(pe, oT_hi_ok, i * G + j)
                    wait(pe, oT_lo_ok, i * G + j)
                for c in range(KC):
                    wait(pe, prob_n_ok, i * G * KC + (j * KC + c + 1))
                    for r in range(R):
                        last = pe.transpose(ps[:, TA + c, r * P:(r + 1) * P], prob_n[:, j % 2, c * R + r, :], ident[:, :])
                    last.then_inc(pe_pT, 1)

            def attend(i, j):
                wait(pe, pT_a_ok, i * G + (j + 1))
                wait(pe, pT_b_ok, i * G + (j + 1))
                for c in range(KC):
                    for r in range(R):
                        h = c * R + r
                        last = pe.matmul(ps[r * D:(r + 1) * D, TA, c * P:(c + 1) * P], v_sb[:, j, h * D:(h + 1) * D],
                                         pT[:, h, :], start=True, stop=True)
                last.then_inc(pe_pv, 1)

            def project(i, j):
                wait(pe, oT_hi_ok, i * G + (j + 1))
                wait(pe, oT_lo_ok, i * G + (j + 1))
                wait(pe, x2_ok, i * G + j)
                split_mm(ps[:, WA, 0:H], [(oT_hi[:, k, :], oT_lo[:, k, :], w_hi[:, 3, k, :], w_lo[:, 3, k, :])
                                          for k in range(KC)]).then_inc(pe_wo, 1)

            def mlp_transpose(m):
                wait(pe, x2_hat_ok, m * G + G)
                transpose_group(x2_hat, pe_x2T)

            def mlp_up(m, v_read):
                wait(pe, x2T_hi_ok, m * KC + KC)
                wait(pe, x2T_lo_ok, m * KC + KC)
                wait(pe, v_ok, v_read)
                for f in range(FC):
                    cols = slice(f * P, (f + 1) * P)
                    if f >= 4:
                        wait(pe, h_hi_ok, m * FC + (f - 3))
                    split_mm(ps[:, UP_BANKS[f % 4], :],
                             [(w1_hi[:, k, cols], w1_lo[:, k, cols], x2T_hi[:, k, :], x2T_lo[:, k, :])
                              for k in range(KC)]).then_inc(pe_w1, 1)

            def mlp_down(m, j, half=None):
                rows = slice(j * P, (j + 1) * P)
                passes = [p for f in range(FC) for p in ((h_hi[:, f, rows], w2_hi[:, f, :]),
                                                         (h_hi[:, f, rows], w2_lo[:, f, :]),
                                                         (h_lo[:, f, rows], w2_hi[:, f, :]))]
                first, end = {None: (0, 3 * FC), 0: (0, 3 * FC // 2), 1: (3 * FC // 2, 3 * FC)}[half]
                if first == 0:
                    wait(pe, h_hi_ok, m * FC + FC)
                    wait(pe, h_lo_ok, m * FC + FC)
                    wait(pe, y_ok, 1 + m * G + j)
                for n in range(first, end):
                    last = pe.matmul(ps[:, WB, 0:H], *passes[n], start=(n == 0), stop=(n == 3 * FC - 1))
                if end == 3 * FC:
                    last.then_inc(pe_w2, 1)

            def body(i, with_mlp):
                m = i - 1
                q_k(i)
                if with_mlp:
                    mlp_transpose(m)
                values(i)
                scores(i, 0)
                if with_mlp:
                    mlp_up(m, i * G + G)
                scores(i, 1)
                for j in range(G):
                    transpose_probs(i, j)
                    if j >= 1:
                        project(i, j - 1)
                    if with_mlp:
                        mlp_down(m, j, 0 if j == G - 1 else None)
                    attend(i, j)
                    if with_mlp and j == G - 1:
                        mlp_down(m, j, 1)
                    if j + 2 < G:
                        scores(i, j + 2)
                project(i, G - 1)

            pe.wait_ge(wa_in, 64)
            pe.wait_ge(vec_in, 16 * 10)
            for n in range(3):
                for c in range(KC):
                    for k in range(KC):
                        pe.matmul(ps[:, 0, n * KC + c:n * KC + c + 1], stage_a[:, n, k, c * P:(c + 1) * P],
                                  b1c[:, k:k + 1], start=(k == 0), stop=(k == KC - 1))
            pe.wait_ge(wb_in, 16)
            for f in range(FC):
                for k in range(KC):
                    last = pe.matmul(ps[:, 0, 8 + f:9 + f], stage_b[:, k, f * P:(f + 1) * P], b2c[:, k:k + 1],
                                     start=(k == 0), stop=(k == KC - 1))
            last.then_inc(bias_mm, 1)
            pe.wait_ge(wide_ready, 1)
            for k in range(KC):
                last = pe.matmul(ps[:, 1, 0:H], v_bias_wide[:, k, :], stage_a[:, 3, k, :], start=(k == 0), stop=(k == KC - 1))
            last.then_inc(orow_mm, 1)
            pe.wait_ge(ident_ready, 2)
            pe.wait_ge(orow_ready, 1)
            pe.wait_ge(w_ready, 7)
            body(0, False)
            pe.wait_ge(w_ready, 11)
            with pe.Fori(1, NG) as i:
                body(i, True)
            pe.wait_ge(x2_ok, NG * G)
            pe.wait_ge(y_ok, 1 + (NG - 1) * G)
            mlp_transpose(NG - 1)
            mlp_up(NG - 1, NG * G)
            for j in range(G):
                mlp_down(NG - 1, j)

        @block.scalar
        def _(act):
            def copy_T(i, hi, mm_done, done):
                for c in range(KC):
                    wait(act, mm_done, i * KC + (c + 1))
                    act.copy(hi[:, c, :], ps[:, TA + c, :]).then_inc(done, 1)

            def q_k(i):
                for n, dst in enumerate((qT, kT)):
                    for c in range(KC):
                        wait(act, pe_qk, i * 4 + (n * KC + c + 1))
                        act.activation(dst[:, c, :], ps[:, n * KC + c, :], ACT.Identity, bias=qkv_bias[:, n, c:c + 1],
                                       scale=(SCALE, 1.0)[n]).then_inc(qk_ok, 1)

            def exps(i, j):
                for c in range(KC):
                    wait(act, neg_max_ok, i * G * KC + (j * KC + c + 1))
                    for h in range(c * R, (c + 1) * R):
                        last = act.activation(prob[:, j % 2, h, :], masked[:, j % 2, h, :], ACT.Exp,
                                              bias=neg_max[:, j % 2, h:h + 1], accum_out=row_sum[:, j % 2, h:h + 1])
                    last.then_inc(exp_ok, 1)

            def probs_T(i, j):
                wait(act, pe_pT, i * G * KC + (j * KC + 1))
                act.copy(pT[:, 0:R, :], ps[:, TA, :].rearrange("p (h q) -> p h q", h=R)).then_inc(pT_a_ok, 1)

            def attn_hi(i, j):
                wait(act, pe_pv, i * G + (j + 1))
                act.copy(oT_hi[:, :, :], ps[:, TA, 0:KC * P].rearrange("p (c q) -> p c q", c=KC)).then_inc(oT_hi_ok, 1)

            def gelus(m):
                for f in range(FC):
                    wait(act, pe_w1, m * FC + (f + 1))
                    if f >= 2:
                        wait(act, h_lo_ok, m * FC + (f - 1))
                    act.activation(h_f32[:, f % 2, :], ps[:, UP_BANKS[f % 4], :], ACT.Gelu,
                                   bias=ff_bias[:, f:f + 1]).then_inc(h_f32_ok, 1)
                    act.activation(h_hi[:, f, :], ps[:, UP_BANKS[f % 4], :], ACT.Gelu,
                                   bias=ff_bias[:, f:f + 1]).then_inc(h_hi_ok, 1)

            def body(i, with_mlp):
                copy_T(i, xT_hi, pe_xT, xT_hi_ok)
                q_k(i)
                if with_mlp:
                    copy_T(i - 1, x2T_hi, pe_x2T, x2T_hi_ok)
                exps(i, 0)
                if with_mlp:
                    gelus(i - 1)
                for j in range(G):
                    probs_T(i, j)
                    if j + 1 < G:
                        exps(i, j + 1)
                    attn_hi(i, j)

            for t, src in ((g1c[:, :], ln1_g), (b1c[:, :], ln1_b), (g2c[:, :], ln2_g), (b2c[:, :], ln2_b), (bqkv[:, 0, :], bq),
                           (bqkv[:, 1, :], bk), (bqkv[:, 2, :], bv), (bff[:, :], b1)):
                act.dma_start(t, src.rearrange("(c p) -> p c", p=P), allow_slow_non_contiguous=True).then_inc(vec_in, 16)
            act.dma_start(bo_row[:, :], bo.partition_broadcast(P)).then_inc(vec_in, 16)
            act.dma_start(b2_row[:, :], b2.partition_broadcast(P)).then_inc(vec_in, 16)
            act.wait_ge(bias_ready, 3)
            body(0, False)
            with act.Fori(1, NG) as i:
                body(i, True)
            copy_T(NG - 1, x2T_hi, pe_x2T, x2T_hi_ok)
            gelus(NG - 1)

        @block.vector
        def _(dve):
            def stats(ln, i, j, src):
                dve.bn_stats(st[ln][:, j, :], src[:, j, :]).then_inc(stats_ok[ln], 1)
                hold_for(dve, stats_ok[ln], i * G + (j + 1), dve_passed)
                dve.bn_aggr(mv[ln][:, j, :], st[ln][:, j, :]).then_inc(mv_ok[ln], 1)

            def rsqrt_var(ln, i, part):
                step = [0 if part == 0 else 5 + 3 * (part - 1)]

                def link(ins):
                    step[0] += 1
                    ins.then_inc(rs_step[ln], 1)
                    wait(dve, rs_step[ln], i * RS_STEPS + step[0])

                y, (ve, nh, a) = rstd[ln], rs_tmp[ln]
                if part == 0:
                    wait(dve, mv_ok[ln], i * G + G)
                    dve.tensor_scalar(neg_mu[ln][:, :], mv[ln][:, :, 0], -1.0, None, ALU.mult).then_inc(rs_step[ln], 1)
                    step[0] += 1
                    link(dve.tensor_scalar(ve[:, :], mv[ln][:, :, 1], EPS, None, ALU.add))
                    link(dve.tensor_scalar(half_bits[:, :], ve[:, :].bitcast(I32), 1, None, ALU.logical_shift_right))
                    link(dve.tensor_scalar(y[:, :].bitcast(I32), half_bits[:, :], -1.0, RSQRT_GUESS, ALU.mult, ALU.add))
                    link(dve.tensor_scalar(nh[:, :], ve[:, :], -0.5, None, ALU.mult))
                else:
                    link(dve.tensor_tensor(a[:, :], y[:, :], y[:, :], ALU.mult))
                    link(dve.tensor_tensor(a[:, :], a[:, :], nh[:, :], ALU.mult))
                    link(dve.scalar_tensor_tensor(out=y[:, :], in0=a[:, :], scalar=1.5, in1=y[:, :],
                                                  op0=ALU.add, op1=ALU.mult))

            def lo_T(i, lo, hi, hi_ok, done):
                for c in range(KC):
                    wait(dve, hi_ok, i * KC + (c + 1))
                    dve.tensor_tensor(lo[:, c, :], ps[:, TA + c, :], hi[:, c, :], ALU.subtract).then_inc(done, 1)

            def values(i):
                for j, bank in enumerate((WA, WB, TA, TB)):
                    wait(dve, pe_v, i * G + (j + 1))
                    dve.tensor_copy(v_sb[:, j, :], ps[:, bank, 0:H]).then_inc(v_ok, 1)

            def maxima(i, j):
                if j == 0:
                    wait(dve, mask_ok, i + 1)
                hold_for(dve, pe_score, i * G + (j + 1), dve_passed)
                for c in range(KC):
                    for r in range(R):
                        h = c * R + r
                        last = dve.tensor_tensor_reduce(masked[:, j % 2, h, :], ps[:, r, c * P:(c + 1) * P], mask[:, j, :],
                                                        1.0, -3.0e38, ALU.add, ALU.max, row_max[:, j % 2, h:h + 1])
                    last.then_inc(max_ok, 1)
                    wait(dve, max_ok, i * G * KC + (j * KC + c + 1))
                    dve.tensor_scalar(neg_max[:, j % 2, c * R:(c + 1) * R], row_max[:, j % 2, c * R:(c + 1) * R], -1.0, None,
                                      ALU.mult).then_inc(neg_max_ok, 1)

            def inverse(i, j, c):
                wait(dve, exp_ok, i * G * KC + (j * KC + c + 1))
                hs = slice(c * R, (c + 1) * R)
                dve.reciprocal(inv_sum[:, j % 2, hs], row_sum[:, j % 2, hs]).then_inc(inv_ok, 1)

            def probs_T(i, j):
                wait(dve, pe_pT, i * G * KC + (j * KC + KC))
                dve.tensor_copy(pT[:, R:2 * R, :], ps[:, TB, :].rearrange("p (h q) -> p h q", h=R)).then_inc(pT_b_ok, 1)

            def attn_lo(i, j):
                wait(dve, oT_hi_ok, i * G + (j + 1))
                dve.tensor_tensor(oT_lo[:, :, :], ps[:, TA, 0:KC * P].rearrange("p (c q) -> p c q", c=KC),
                                  oT_hi[:, :, :], ALU.subtract).then_inc(oT_lo_ok, 1)

            def residual(i, j):
                wait(dve, pe_wo, i * G + (j + 1))
                if j == 0:
                    wait(dve, x_res_ok, i * G + G)
                    wait(dve, x2_hat_ok, i * G)
                    wait(dve, x2_res_ok, i * G)
                dve.tensor_tensor(x2[:, j, :], ps[:, WA, 0:H], x_res[:, j, :], ALU.add).then_inc(x2_ok, 1)
                wait(dve, x2_ok, i * G + (j + 1))
                stats(1, i, j, x2)

            def gelu_lo(m, meanwhile=lambda f: None):
                for f in range(FC):
                    wait(dve, h_hi_ok, m * FC + (f + 1))
                    dve.tensor_tensor(h_lo[:, f, :], h_f32[:, f % 2, :], h_hi[:, f, :], ALU.subtract).then_inc(h_lo_ok, 1)
                    meanwhile(f)

            def finish(m, j):
                wait(dve, pe_w2, m * G + (j + 1))
                wait(dve, x2_res_ok, m * G + (j + 1))
                wait(dve, y_stored, 1 + m * G * 16)
                dve.tensor_tensor(y_out[:, j, :], ps[:, WB, 0:H], x2_res[:, j, :], ALU.add).then_inc(y_ok, 1)

            def ln1_stats(i, j):
                if j == 0:
                    wait(dve, x_loaded, (i + 1) * 16)
                    wait(dve, x_hat_ok, i * G)
                stats(0, i, j, x_in)

            def next_ln1(i, f):
                if f < G:
                    ln1_stats(i + 1, f)
                else:
                    rsqrt_var(0, i + 1, f - G)

            def body(i, with_mlp, with_next):
                m = i - 1
                lo_T(i, xT_lo, xT_hi, xT_hi_ok, xT_lo_ok)
                if with_mlp:
                    for part in range(RS_PARTS):
                        rsqrt_var(1, m, part)
                    lo_T(m, x2T_lo, x2T_hi, x2T_hi_ok, x2T_lo_ok)
                values(i)
                maxima(i, 0)
                for c in range(KC):
                    inverse(i, 0, c)
                meanwhile = (lambda f: next_ln1(i, f)) if with_next else (lambda f: None)
                if with_mlp:
                    gelu_lo(m, meanwhile)
                else:
                    for f in range(FC):
                        meanwhile(f)
                maxima(i, 1)
                for j in range(G):
                    probs_T(i, j)
                    if j >= 1:
                        residual(i, j - 1)
                    if j + 1 < G:
                        inverse(i, j + 1, 0)
                    if with_mlp and j < G - 1:
                        finish(m, j)
                    if j + 1 < G:
                        inverse(i, j + 1, 1)
                    attn_lo(i, j)
                    if with_mlp and j == G - 1:
                        finish(m, j)
                    if j + 2 < G:
                        maxima(i, j + 2)
                residual(i, G - 1)

            for j in range(G):
                ln1_stats(0, j)
            for part in range(RS_PARTS):
                rsqrt_var(0, 0, part)
            dve.wait_ge(wa_in, 64)
            dve.wait_ge(vec_in, 16 * 10)
            for n in range(3):
                for k in range(KC):
                    dve.tensor_scalar(w_hi[:, n, k, :], stage_a[:, n, k, :], g1c[:, k:k + 1], None, ALU.mult).then_inc(fold, 1)
            dve.tensor_copy(w_hi[:, 3, :, :], stage_a[:, 3, :, :]).then_inc(fold, 1)
            dve.wait_ge(fold, 7)
            for n in range(3):
                for k in range(KC):
                    dve.scalar_tensor_tensor(out=w_lo[:, n, k, :], in0=stage_a[:, n, k, :], scalar=g1c[:, k:k + 1],
                                             in1=w_hi[:, n, k, :], op0=ALU.mult, op1=ALU.subtract).then_inc(w_ready, 1)
            dve.tensor_tensor(w_lo[:, 3, :, :], stage_a[:, 3, :, :], w_hi[:, 3, :, :], ALU.subtract).then_inc(w_ready, 1)
            dve.wait_ge(bias_mm, 1)
            dve.tensor_tensor(qkv_bias[:, :, :], ps[:, 0, 0:3 * KC].rearrange("p (n c) -> p n c", n=3), bqkv[:, :, :],
                              ALU.add).then_inc(bias_ready, 1)
            dve.tensor_tensor(ff_bias[:, :], ps[:, 0, 8:8 + FC], bff[:, :], ALU.add).then_inc(bias_ready, 1)
            dve.wait_ge(bias_ready, 2)
            dve.tensor_scalar(qkv_bias[:, 0, :], qkv_bias[:, 0, :], SCALE, None, ALU.mult).then_inc(bias_ready, 1)
            dve.tensor_copy(v_bias_wide[:, :, :], qkv_bias[:, 2, :].unsqueeze(2).broadcast_to([P, KC, P])).then_inc(wide_ready, 1)
            dve.wait_ge(orow_mm, 1)
            dve.tensor_tensor(o_bias_row[:, :], ps[:, 1, 0:H], bo_row[:, :], ALU.add).then_inc(orow_ready, 1)
            dve.wait_ge(wb_in, 16)
            for k in range(KC):
                dve.tensor_scalar(w1_hi[:, k, :], stage_b[:, k, :], g2c[:, k:k + 1], None, ALU.mult).then_inc(fold, 1)
            dve.wait_ge(wc_in, 16)
            for k in range(2):
                half = slice(k * FC // 2, (k + 1) * FC // 2)
                dve.tensor_copy(w2_hi[:, half, :], stage_c[:, half, :]).then_inc(fold, 1)
            dve.wait_ge(fold, 11)
            for k in range(KC):
                dve.scalar_tensor_tensor(out=w1_lo[:, k, :], in0=stage_b[:, k, :], scalar=g2c[:, k:k + 1],
                                         in1=w1_hi[:, k, :], op0=ALU.mult, op1=ALU.subtract).then_inc(w_ready, 1)
            for k in range(2):
                half = slice(k * FC // 2, (k + 1) * FC // 2)
                dve.tensor_tensor(w2_lo[:, half, :], stage_c[:, half, :], w2_hi[:, half, :], ALU.subtract).then_inc(w_ready, 1)
            body(0, False, True)
            with dve.Fori(1, NG - 1) as i:
                body(i, True, True)
            body(NG - 1, True, False)
            for part in range(RS_PARTS):
                rsqrt_var(1, NG - 1, part)
            lo_T(NG - 1, x2T_lo, x2T_hi, x2T_hi_ok, x2T_lo_ok)
            gelu_lo(NG - 1)
            for j in range(G):
                finish(NG - 1, j)

        @block.gpsimd
        def _(pool):
            def hold(sem, value):
                hold_for(pool, sem, value, pool_passed)

            def make_mask(i):
                hold(adj_loaded, (i + 1) * 16)
                hold(max_ok, i * G * KC)
                nc.gpsimd.tensor_scalar(mask[:, :, :], adj_in[:, :, :], MASKED, -MASKED, ALU.mult, ALU.add).then_inc(mask_ok, 1)

            def apply_ln(ln, i, dst, src, done):
                hold(rs_step[ln], (i + 1) * RS_STEPS)
                for j in range(G):
                    nc.gpsimd.tensor_scalar(dst[:, j, :], src[:, j, :], neg_mu[ln][:, j:j + 1], rstd[ln][:, j:j + 1],
                                            ALU.add, ALU.mult).then_inc(done, 1)

            def ln1(i):
                hold(pe_xT, i * KC)
                apply_ln(0, i, x_hat, x_in, x_hat_ok)

            def add_o_bias(i, j):
                wait(pool, x2_ok, i * G + (j - G + 1))
                nc.gpsimd.tensor_tensor(x_res[:, j, :], x_in[:, j, :], o_bias_row[:, :], ALU.add).then_inc(x_res_ok, 1)

            def normalise(i, j):
                for c in range(KC):
                    wait(pool, inv_ok, i * G * KC + (j * KC + c + 1))
                    hs = slice(c * R, (c + 1) * R)
                    nc.gpsimd.tensor_tensor(prob_n[:, j % 2, hs, :], prob[:, j % 2, hs, :],
                                            inv_sum[:, j % 2, hs].unsqueeze(2).broadcast_to([P, R, S]), ALU.mult).then_inc(prob_n_ok, 1)

            def add_b2(i, j):
                wait(pool, x2_ok, i * G + (j + 1))
                wait(pool, y_ok, 1 + i * G + (j - G + 1))
                nc.gpsimd.tensor_tensor(x2_res[:, j, :], x2[:, j, :], b2_row[:, :], ALU.add).then_inc(x2_res_ok, 1)

            def body(i, with_next):
                normalise(i, 0)
                normalise(i, 1)
                if with_next:
                    ln1(i + 1)
                normalise(i, 2)
                add_b2(i, 0)
                if with_next:
                    add_o_bias(i + 1, 0)
                normalise(i, 3)
                if with_next:
                    make_mask(i + 1)
                for j in range(1, G):
                    add_b2(i, j)
                    if with_next:
                        add_o_bias(i + 1, j)
                hold(pe_x2T, i * KC)
                apply_ln(1, i, x2_hat, x2, x2_hat_ok)

            nc.gpsimd.memset(ident[:, :], 0.0).then_inc(ident_ready, 1)
            pool.wait_ge(ident_ready, 1)
            nc.gpsimd.affine_select(out=ident[:, :], in_=ident[:, :], compare_op=ALU.not_equal, fill=1.0, base=0,
                                    pattern=[[-1, P]], channel_multiplier=1).then_inc(ident_ready, 1)
            ln1(0)
            make_mask(0)
            pool.wait_ge(orow_ready, 1)
            for j in range(G):
                add_o_bias(0, j)
            body(0, True)
            with pool.Fori(1, NG - 1) as i:
                body(i, True)
            body(NG - 1, False)


_INS = ["x", "adj"] + ["L0_gnn_" + n for n in ("ln1_g", "ln1_b", "ln2_g", "ln2_b", "Wq", "bq", "Wk", "bk", "Wv", "bv",
                                               "Wo", "bo", "W1", "b1", "W2", "b2")]


def kernel(**inputs):
    import numpy as _np
    import concourse.bacc as _bacc
    from concourse import mybir as _mybir
    from concourse.bass_utils import run_bass_kernel_spmd as _run

    nc = _bacc.Bacc("TRN2", target_bir_lowering=False, num_devices=1)
    arrays, args = {}, []
    for name in _INS:
        a = _np.ascontiguousarray(inputs[name])
        arrays[f"in_{name}"] = a
        args.append(nc.dram_tensor(f"in_{name}", a.shape, _mybir.dt.from_np(a.dtype), kind="ExternalInput").ap())
    out = nc.dram_tensor("out_0", arrays["in_x"].shape, _mybir.dt.float32, kind="ExternalOutput").ap()
    graph_layer(nc, *args, out)
    r = _run(nc, [arrays], core_ids=[0])
    return r.results[0]["out_0"]
```

```python
from contextlib import ExitStack

import concourse.bass as bass
from concourse import mybir

F32 = mybir.dt.float32
F32R = mybir.dt.float32r
I32 = mybir.dt.int32
U8 = mybir.dt.uint8
ALU = mybir.AluOpType
ACT = mybir.ActivationFunctionType

P = 128
G = 4
HEADS = 8
EPS = 1e-5
MASKED = 1e30
RSQRT_GUESS = 1597463007.0
NEWTON = 3
RS_PARTS = 1 + NEWTON
RS_STEPS = 5 + 3 * NEWTON
BANK_COLS = 512

TA, TB, WA, WB = 4, 5, 6, 7
XT = 2
UP_BANKS = (WA, WB, TA, TB, 0, 1, 2, 3)

V_BANKS = (TA, TB, WA, WB)
LAST_BANKS = (WA, WB, TA, TB)


def wait(eng, sem, value):
    if isinstance(value, int) and value <= 0:
        return
    eng.wait_ge(sem, value)


def done_before(m, per_group, half):
    return m * per_group + (per_group if half == 1 else 0)


def graphs_of(half):
    return range(G) if half is None else range(2 * half, 2 * half + 2)


def nodes_of(half):
    return slice(graphs_of(half)[0] * P, (graphs_of(half)[-1] + 1) * P)


def up_bank(f, half):
    return UP_BANKS[(f + (half == 1)) % len(UP_BANKS)]


def hold_for(eng, sem, value, passed):
    if isinstance(value, int):
        return wait(eng, sem, value)
    eng.wait_ge(sem, value)
    eng.sem_inc(passed, 1)


def graph_layer(nc, x, adj, ln1_g, ln1_b, ln2_g, ln2_b, Wq, bq, Wk, bk, Wv, bv, Wo, bo, W1, b1, W2, b2, out):
    B, S, H = x.shape
    FF = W1.shape[1]
    NG = B // G
    D = H // HEADS
    KC = H // P
    FC = FF // P
    R = P // D
    TOK = G * P
    SCALE = float(D) ** -0.5
    assert S == P and D == 32 and TOK == BANK_COLS and KC == 2

    with ExitStack() as ctx:
        def sb(name, shape, dt=F32):
            return ctx.enter_context(nc.sbuf_tensor(name, shape, dt))

        def sem(name):
            return ctx.enter_context(nc.semaphore(name))

        ps = ctx.enter_context(nc.psum_tensor("ps", [P, 8, BANK_COLS], F32))

        w_hi = sb("w_hi", [P, 4, KC, H], F32R)
        w_lo = sb("w_lo", [P, 4, KC, H], F32R)
        w1_hi = sb("w1_hi", [P, KC, FF], F32R)
        w1_lo = sb("w1_lo", [P, KC, FF], F32R)
        w2_hi = sb("w2_hi", [P, FC, H], F32R)
        w2_lo = sb("w2_lo", [P, FC, H], F32R)
        stage_a = sb("stage_a", [P, 4, KC, H])
        stage_b = sb("stage_b", [P, KC, FF])
        stage_c = sb("stage_c", [P, FC, H])
        g1c, b1c, g2c, b2c = (sb(n, [P, KC]) for n in ("g1c", "b1c", "g2c", "b2c"))
        bqkv = sb("bqkv", [P, 3, KC])
        bff = sb("bff", [P, FC])
        qkv_bias = sb("qkv_bias", [P, 3, KC])
        ff_bias = sb("ff_bias", [P, FC])
        v_bias_wide = sb("v_bias_wide", [P, KC, P])
        bo_row = sb("bo_row", [P, H])
        b2_row = sb("b2_row", [P, H])
        o_bias_row = sb("o_bias_row", [P, H])
        ident = sb("ident", [P, P])

        x_in = sb("x_in", [P, G, H])
        adj_in = sb("adj_in", [P, G, S], U8)
        mask = sb("mask", [P, G, S])
        x_res = sb("x_res", [P, G, H])
        x_hat = sb("x_hat", [P, G, H])
        xT_hi = sb("xT_hi", [P, KC, TOK], F32R)
        xT_lo = sb("xT_lo", [P, KC, TOK], F32R)
        qT = sb("qT", [P, KC, TOK])
        kT = sb("kT", [P, KC, TOK])
        v_sb = sb("v_sb", [P, G, H])
        masked = sb("masked", [P, 2, HEADS, S])
        row_max = sb("row_max", [P, 2, HEADS])
        neg_max = sb("neg_max", [P, 2, HEADS])
        prob = sb("prob", [P, 2, HEADS, S])
        row_sum = sb("row_sum", [P, 2, HEADS])
        inv_sum = sb("inv_sum", [P, 2, HEADS])
        prob_n = sb("prob_n", [P, 2, HEADS, S])
        pT = sb("pT", [P, HEADS, S])
        oT_hi = sb("oT_hi", [P, KC, P], F32R)
        oT_lo = sb("oT_lo", [P, KC, P], F32R)
        x2 = sb("x2", [P, G, H])
        x2_res = sb("x2_res", [P, G, H])
        x2_hat = sb("x2_hat", [P, G, H])
        x2T_hi = sb("x2T_hi", [P, KC, TOK], F32R)
        x2T_lo = sb("x2T_lo", [P, KC, TOK], F32R)
        h_f32 = sb("h_f32", [P, 4, TOK])
        h_hi = sb("h_hi", [P, FC, TOK], F32R)
        h_lo = sb("h_lo", [P, FC, TOK], F32R)
        y_out = sb("y_out", [P, G, H])
        st = [sb(f"st{n}", [P, G, 6]) for n in (1, 2)]
        mv = [sb(f"mv{n}", [P, G, 2]) for n in (1, 2)]
        neg_mu = [sb(f"neg_mu{n}", [P, G]) for n in (1, 2)]
        rstd = [sb(f"rstd{n}", [P, G]) for n in (1, 2)]
        rs_tmp = [[sb(f"rs_{t}{n}", [P, G]) for t in ("var_eps", "neg_half", "a")] for n in (1, 2)]
        half_bits = sb("half_bits", [P, G], I32)

        wa_in = [sem(f"wa_in{n}") for n in range(4)]
        wb_in, wc_in, vec1_in, vec2_in, bo_in = (sem(n) for n in ("wb_in", "wc_in", "vec1_in", "vec2_in", "bo_in"))
        x_loaded, adj_loaded, y_stored = (sem(n) for n in ("x_loaded", "adj_loaded", "y_stored"))
        ident_ready, bias_mm, bias_ready, wide_ready, orow_mm, orow_ready, ff_mm, ff_bias_ready = (
            sem(n) for n in ("ident_ready", "bias_mm", "bias_ready", "wide_ready", "orow_mm", "orow_ready",
                             "ff_mm", "ff_bias_ready"))
        w_hi_ok, w_lo_ok, w1_hi_ok, w2_hi_ok, ff_lo_ok = (
            sem(n) for n in ("w_hi_ok", "w_lo_ok", "w1_hi_ok", "w2_hi_ok", "ff_lo_ok"))
        pe_xT, pe_qk, pe_v, pe_score, pe_pT, pe_pv, pe_wo, pe_x2T, pe_w1, pe_w2 = (
            sem(n) for n in ("pe_xT", "pe_qk", "pe_v", "pe_score", "pe_pT", "pe_pv", "pe_wo", "pe_x2T",
                             "pe_w1", "pe_w2"))
        xT_hi_ok, qk_ok, v_b_ok, exp_ok, x2T_hi_ok, h_hi_ok, pT_a_ok, oT_hi_ok = (
            sem(n) for n in ("xT_hi_ok", "qk_ok", "v_b_ok", "exp_ok", "x2T_hi_ok", "h_hi_ok", "pT_a_ok",
                             "oT_hi_ok"))
        xT_lo_ok, v_a_ok, max_ok, neg_max_ok, inv_ok, x2T_lo_ok, h_lo_ok, pT_b_ok, oT_lo_ok, x2_ok, y_ok = (
            sem(n) for n in ("xT_lo_ok", "v_a_ok", "max_ok", "neg_max_ok", "inv_ok", "x2T_lo_ok", "h_lo_ok",
                             "pT_b_ok", "oT_lo_ok", "x2_ok", "y_ok"))
        x2_hat_b_ok = sem("x2_hat_b_ok")
        stats_ok = [sem(f"stats{n}_ok") for n in (1, 2)]
        mv_ok = [sem(f"mv{n}_ok") for n in (1, 2)]
        rs_step = [sem(f"rs_step{n}") for n in (1, 2)]
        prob_n_ok, x_hat_ok, x_res_ok, x2_res_ok, x2_hat_a_ok, mask_ok = (
            sem(n) for n in ("prob_n_ok", "x_hat_ok", "x_res_ok", "x2_res_ok", "x2_hat_a_ok", "mask_ok"))

        pool_passed, dve_passed = sem("pool_passed"), sem("dve_passed")

        block = ctx.enter_context(nc.Block())

        @block.sync
        def _(sp):
            def load_group(i, first_graph):
                wait(sp, x_hat_ok, i * G)
                wait(sp, x_res_ok, i * G)
                wait(sp, mask_ok, i)
                sp.dma_start(x_in[:, :, :], x[bass.ds(first_graph, G)].rearrange("g p d -> p g d")).then_inc(x_loaded, 16)
                sp.dma_start(adj_in[:, :, :], adj[bass.ds(first_graph, G)].rearrange("g p d -> p g d")).then_inc(adj_loaded, 16)

            def store_group(m, first_graph):
                for j in range(G):
                    wait(sp, y_ok, 1 + m * G + (j + 1))
                    sp.dma_start(out[bass.ds(first_graph + j, 1)].rearrange("g p d -> p (g d)"),
                                 y_out[:, j, :]).then_inc(y_stored, 16)

            def load_weight(dst, src, done):
                sp.dma_start(dst, src.rearrange("(c p) n -> p c n", p=P)).then_inc(done, 16)

            sp.sem_inc(y_stored, 1)
            sp.sem_inc(y_ok, 1)
            sp.dma_start(x_in[:, :, :], x[0:G].rearrange("g p d -> p g d")).then_inc(x_loaded, 16)
            for n, w in enumerate((Wq, Wk, Wv, Wo)):
                load_weight(stage_a[:, n, :, :], w, wa_in[n])
            sp.dma_start(bo_row[:, :], bo.partition_broadcast(P)).then_inc(bo_in, 16)
            sp.dma_start(adj_in[:, :, :], adj[0:G].rearrange("g p d -> p g d")).then_inc(adj_loaded, 16)
            load_weight(stage_b[:, :, :], W1, wb_in)
            load_weight(stage_c[:, :, :], W2, wc_in)
            load_group(1, G)
            with sp.Fori(1, NG - 1) as i:
                ahead = sp.snap(i * G + G)
                behind = [sp.snap(i * G - G + j) for j in range(G)]
                load_group(i + 1, ahead)
                for j in range(G):
                    sp.wait_ge(y_ok, 1 + i * G - G + (j + 1))
                    sp.dma_start(out[bass.ds(behind[j], 1)].rearrange("g p d -> p (g d)"),
                                 y_out[:, j, :]).then_inc(y_stored, 16)
            store_group(NG - 2, (NG - 2) * G)
            store_group(NG - 1, (NG - 1) * G)
            sp.wait_ge(y_stored, 1 + 16 * B)

        @block.tensor
        def _(pe):
            def split_mm(dst, pairs, before_lo=lambda: None):
                passes = [p for sh, sl, mh, ml in pairs for p in ((sh, mh), (sl, mh))]
                passes += [(sh, ml) for sh, sl, mh, ml in pairs]
                for n, (s, m) in enumerate(passes):
                    if n == 2 * len(pairs):
                        before_lo()
                    last = pe.matmul(dst, s, m, start=(n == 0), stop=(n == len(passes) - 1))
                return last

            def transpose_group(src, bank, done, graphs=range(G)):
                for c in range(KC):
                    for j in graphs:
                        last = pe.transpose(ps[:, bank + c, j * P:(j + 1) * P], src[:, j, c * P:(c + 1) * P], ident[:, :])
                    last.then_inc(done, 1)

            def transpose_x(i):
                wait(pe, x_hat_ok, i * G + G)
                wait(pe, max_ok, i * G * KC)
                transpose_group(x_hat, XT, pe_xT)

            def q_k(i, products):
                for b in products:
                    n, c = divmod(b, KC)
                    cols = slice(c * P, (c + 1) * P)
                    if b == 0:
                        wait(pe, xT_hi_ok, i * KC + KC)
                        wait(pe, max_ok, i * G * KC)
                    split_mm(ps[:, b, :],
                             [(w_hi[:, n, k, cols], w_lo[:, n, k, cols], xT_hi[:, k, :], xT_lo[:, k, :])
                              for k in range(KC)], lambda: wait(pe, xT_lo_ok, i * KC + KC)).then_inc(pe_qk, 1)

            def values(i, graphs):
                for j in graphs:
                    if j == 2:
                        wait(pe, x2_ok, i * G)
                    if j == 3:
                        wait(pe, y_ok, 1 + i * G - G)
                        wait(pe, orow_ready, 1)
                    rows = slice(j * P, (j + 1) * P)
                    split_mm(ps[:, V_BANKS[j], 0:H],
                             [(xT_hi[:, k, rows], xT_lo[:, k, rows], w_hi[:, 2, k, :], w_lo[:, 2, k, :])
                              for k in range(KC)]).then_inc(pe_v, 1)

            def scores(i, j):
                if j == 0:
                    wait(pe, qk_ok, i * 4 + 4)
                else:
                    wait(pe, max_ok, i * G * KC + j * KC)
                    if j == 2:
                        wait(pe, h_hi_ok, i * FC)
                rows = slice(j * P, (j + 1) * P)
                for c in range(KC):
                    for r in range(R):
                        part = slice(r * D, (r + 1) * D)
                        last = pe.matmul(ps[:, r, c * P:(c + 1) * P], qT[part, c, rows], kT[part, c, rows],
                                         start=True, stop=True)
                last.then_inc(pe_score, 1)

            def transpose_probs(i, j, chunks=range(KC)):
                if chunks[0] > 0:
                    pass
                elif j == 0:
                    wait(pe, v_a_ok, i * 2 + 2)
                    wait(pe, v_b_ok, i * 2 + 2)
                    wait(pe, h_hi_ok, i * FC - 4)
                else:
                    wait(pe, oT_hi_ok, i * G + j)
                    wait(pe, oT_lo_ok, i * G + j)
                for c in chunks:
                    wait(pe, prob_n_ok, i * G * KC + (j * KC + c + 1))
                    for r in range(R):
                        last = pe.transpose(ps[:, TA + c, r * P:(r + 1) * P], prob_n[:, j % 2, c * R + r, :], ident[:, :])
                    last.then_inc(pe_pT, 1)

            def attend(i, j):
                wait(pe, pT_a_ok, i * G + (j + 1))
                wait(pe, pT_b_ok, i * G + (j + 1))
                for c in range(KC):
                    for r in range(R):
                        h = c * R + r
                        last = pe.matmul(ps[r * D:(r + 1) * D, TA, c * P:(c + 1) * P], v_sb[:, j, h * D:(h + 1) * D],
                                         pT[:, h, :], start=True, stop=True)
                last.then_inc(pe_pv, 1)

            def project(i, j):
                wait(pe, oT_hi_ok, i * G + (j + 1))
                wait(pe, oT_lo_ok, i * G + (j + 1))
                wait(pe, x2_ok, i * G + j)
                split_mm(ps[:, WA, 0:H], [(oT_hi[:, k, :], oT_lo[:, k, :], w_hi[:, 3, k, :], w_lo[:, 3, k, :])
                                          for k in range(KC)]).then_inc(pe_wo, 1)

            def mlp_transpose(m, v_read, half=None):
                wait(pe, v_a_ok, v_read)
                if half != 1:
                    wait(pe, x2_hat_a_ok, m * 2 + 2)
                if half != 0:
                    wait(pe, x2_hat_b_ok, m * 2 + 2)
                if half == 1:
                    wait(pe, h_hi_ok, m * FC + 4)
                transpose_group(x2_hat, TA, pe_x2T, graphs_of(half))

            def mlp_up(m, v_read, scores_read, half=None):
                nodes = nodes_of(half)
                wait(pe, x2T_hi_ok, done_before(m, KC, half) + KC)
                wait(pe, v_b_ok, v_read)
                for f in range(FC):
                    cols = slice(f * P, (f + 1) * P)
                    if f == 4:
                        wait(pe, max_ok, scores_read)
                    if half == 1:
                        if f < FC - 1:
                            wait(pe, h_hi_ok, m * FC + (f + 2))
                        else:
                            wait(pe, y_ok, 1 + m * G + 1)
                    split_mm(ps[:, up_bank(f, half), nodes],
                             [(w1_hi[:, k, cols], w1_lo[:, k, cols], x2T_hi[:, k, nodes], x2T_lo[:, k, nodes])
                              for k in range(KC)],
                             lambda: wait(pe, x2T_lo_ok, done_before(m, KC, half) + KC)).then_inc(pe_w1, 1)

            def down_passes(rows):
                return [p for f in range(FC) for p in ((h_hi[:, f, rows], w2_hi[:, f, :]),
                                                       (h_hi[:, f, rows], w2_lo[:, f, :]),
                                                       (h_lo[:, f, rows], w2_hi[:, f, :]))]

            def mlp_down(m, j, half=None):
                passes = down_passes(slice(j * P, (j + 1) * P))
                first, end = {None: (0, 3 * FC), 0: (0, 3 * FC // 2), 1: (3 * FC // 2, 3 * FC)}[half]
                if first == 0:
                    wait(pe, y_ok, 1 + m * G + j)
                    if j == 0:
                        wait(pe, h_hi_ok, m * FC + 2)
                for n in range(first, end):
                    if j == 0 and n % 3 == 0:
                        wait(pe, h_hi_ok, m * FC + (n // 3 + 1))
                    if j == 0 and n % 3 == 2:
                        wait(pe, h_lo_ok, m * FC + (n // 3 + 1))
                    last = pe.matmul(ps[:, WB, 0:H], *passes[n], start=(n == 0), stop=(n == 3 * FC - 1))
                if end == 3 * FC:
                    last.then_inc(pe_w2, 1)

            def last_mlp_down(j):
                m, half = NG - 1, j // 2
                hidden = done_before(m, FC, half)
                bank = LAST_BANKS[j]
                if j > 0:
                    wait(pe, h_hi_ok, done_before(m, FC, 1) + j)
                passes = down_passes(slice(j * P, (j + 1) * P))
                for n, (stationary, moving) in enumerate(passes):
                    if j % 2 == 0 and n % 3 == 0:
                        wait(pe, h_hi_ok, hidden + (n // 3 + 1))
                    if j % 2 == 0 and n % 3 == 2:
                        wait(pe, h_lo_ok, hidden + (n // 3 + 1))
                    last = pe.matmul(ps[:, bank, 0:H], stationary, moving, start=(n == 0), stop=(n == 3 * FC - 1))
                last.then_inc(pe_w2, 1)

            def o_bias():
                pe.wait_ge(wide_ready, 1)
                pe.wait_ge(wa_in[3], 16)
                for k in range(KC):
                    last = pe.matmul(ps[:, WB, 0:H], v_bias_wide[:, k, :], stage_a[:, 3, k, :], start=(k == 0), stop=(k == KC - 1))
                last.then_inc(orow_mm, 1)

            def ff_bias_products():
                pe.wait_ge(v_b_ok, 2)
                pe.wait_ge(wb_in, 16)
                pe.wait_ge(vec2_in, 16 * 3)
                for f in range(FC):
                    for k in range(KC):
                        last = pe.matmul(ps[:, WB, f:f + 1], stage_b[:, k, f * P:(f + 1) * P], b2c[:, k:k + 1],
                                         start=(k == 0), stop=(k == KC - 1))
                last.then_inc(ff_mm, 1)

            def body(i, with_mlp, with_next):
                m = i - 1

                def down(j, half=None):
                    if with_mlp:
                        mlp_down(m, j, half)

                q_k(i, (0,))
                if with_mlp:
                    project(m, G - 1)
                q_k(i, (1, 2, 3))
                if not with_mlp:
                    o_bias()
                values(i, (0, 1))
                scores(i, 0)
                values(i, (2, 3))
                if with_mlp:
                    mlp_transpose(m, i * 2 + 2)
                scores(i, 1)
                if with_mlp:
                    mlp_up(m, i * 2 + 2, i * G * KC + 2 * KC)
                else:
                    ff_bias_products()
                transpose_probs(i, 0)
                down(0)
                attend(i, 0)
                scores(i, 2)
                down(1)
                transpose_probs(i, 1)
                project(i, 0)
                down(2, 0)
                attend(i, 1)
                scores(i, 3)
                transpose_probs(i, 2)
                project(i, 1)
                down(2, 1)
                attend(i, 2)
                down(3, 0)
                transpose_probs(i, 3, (0,))
                project(i, 2)
                if with_next:
                    transpose_x(i + 1)
                transpose_probs(i, 3, (1,))
                down(3, 1)
                attend(i, 3)

            def qkv_bias_products(n):
                pe.wait_ge(wa_in[n], 16)
                for c in range(KC):
                    for k in range(KC):
                        last = pe.matmul(ps[:, TA, n * KC + c:n * KC + c + 1], stage_a[:, n, k, c * P:(c + 1) * P],
                                         b1c[:, k:k + 1], start=(k == 0), stop=(k == KC - 1))
                last.then_inc(bias_mm, 1)

            pe.wait_ge(vec1_in, 16 * 6)
            qkv_bias_products(0)
            qkv_bias_products(1)
            pe.wait_ge(ident_ready, 2)
            transpose_x(0)
            qkv_bias_products(2)
            pe.wait_ge(w_lo_ok, 4 * KC)
            pe.wait_ge(bias_ready, 1)
            body(0, False, True)
            pe.wait_ge(ff_lo_ok, KC + 2)
            pe.wait_ge(ff_bias_ready, 1)
            with pe.Fori(1, NG - 1) as i:
                body(i, True, True)
            body(NG - 1, True, False)
            project(NG - 1, G - 1)
            mlp_transpose(NG - 1, NG * 2, 0)
            pe.wait_ge(x2_ok, NG * G)
            pe.wait_ge(y_ok, 1 + (NG - 1) * G)
            mlp_up(NG - 1, NG * 2, NG * G * KC, 0)
            mlp_transpose(NG - 1, NG * 2, 1)
            last_mlp_down(0)
            mlp_up(NG - 1, NG * 2, NG * G * KC, 1)
            for j in range(1, G):
                last_mlp_down(j)

        @block.scalar
        def _(act):
            def copy_T(i, hi, bank, mm_done, done, half=None):
                for c in range(KC):
                    wait(act, mm_done, done_before(i, KC, half) + (c + 1))
                    act.copy(hi[:, c, nodes_of(half)], ps[:, bank + c, nodes_of(half)]).then_inc(done, 1)

            def q_k(i):
                for n, dst in enumerate((qT, kT)):
                    for c in range(KC):
                        wait(act, pe_qk, i * 4 + (n * KC + c + 1))
                        act.activation(dst[:, c, :], ps[:, n * KC + c, :], ACT.Identity, bias=qkv_bias[:, n, c:c + 1],
                                       scale=(SCALE, 1.0)[n]).then_inc(qk_ok, 1)

            def values(i):
                for j in (2, 3):
                    wait(act, pe_v, i * G + (j + 1))
                    act.copy(v_sb[:, j, :], ps[:, V_BANKS[j], 0:H]).then_inc(v_b_ok, 1)

            def exps(i, j, chunks=range(KC)):
                for c in chunks:
                    wait(act, neg_max_ok, i * G * KC + (j * KC + c + 1))
                    for h in range(c * R, (c + 1) * R):
                        last = act.activation(prob[:, j % 2, h, :], masked[:, j % 2, h, :], ACT.Exp,
                                              bias=neg_max[:, j % 2, h:h + 1], accum_out=row_sum[:, j % 2, h:h + 1])
                    last.then_inc(exp_ok, 1)

            def probs_T(i, j):
                wait(act, pe_pT, i * G * KC + (j * KC + 1))
                act.copy(pT[:, 0:R, :], ps[:, TA, :].rearrange("p (h q) -> p h q", h=R)).then_inc(pT_a_ok, 1)

            def attn_hi(i, j):
                wait(act, pe_pv, i * G + (j + 1))
                act.copy(oT_hi[:, :, :], ps[:, TA, 0:KC * P].rearrange("p (c q) -> p c q", c=KC)).then_inc(oT_hi_ok, 1)

            def gelus(m, half=None):
                nodes = nodes_of(half)
                for f in range(FC):
                    chunk = done_before(m, FC, half) + f
                    wait(act, pe_w1, chunk + 1)
                    if f >= 4 or half == 1:
                        wait(act, h_lo_ok, chunk - 3)
                    act.activation(h_f32[:, f % 4, nodes], ps[:, up_bank(f, half), nodes], ACT.Gelu,
                                   bias=ff_bias[:, f:f + 1])
                    act.activation(h_hi[:, f, nodes], ps[:, up_bank(f, half), nodes], ACT.Gelu,
                                   bias=ff_bias[:, f:f + 1]).then_inc(h_hi_ok, 1)

            def body(i, with_mlp, with_next):
                q_k(i)
                values(i)
                if with_mlp:
                    copy_T(i - 1, x2T_hi, TA, pe_x2T, x2T_hi_ok)
                exps(i, 0)
                if with_mlp:
                    gelus(i - 1)
                    probs_T(i, 0)
                    exps(i, 1, (0,))
                    attn_hi(i, 0)
                    exps(i, 1, (1,))
                else:
                    exps(i, 1)
                    probs_T(i, 0)
                    attn_hi(i, 0)
                    probs_T(i, 1)
                exps(i, 2)
                if with_mlp:
                    probs_T(i, 1)
                attn_hi(i, 1)
                probs_T(i, 2)
                exps(i, 3, (0,))
                attn_hi(i, 2)
                exps(i, 3, (1,))
                probs_T(i, 3)
                if with_next:
                    copy_T(i + 1, xT_hi, XT, pe_xT, xT_hi_ok)
                attn_hi(i, 3)

            def load_columns(pairs, done):
                for t, src in pairs:
                    act.dma_start(t, src.rearrange("(c p) -> p c", p=P), allow_slow_non_contiguous=True).then_inc(done, 16)

            load_columns(((g1c[:, :], ln1_g), (b1c[:, :], ln1_b), (bqkv[:, 0, :], bq), (bqkv[:, 1, :], bk), (bqkv[:, 2, :], bv),
                          (g2c[:, :], ln2_g)), vec1_in)
            act.wait_ge(vec1_in, 16 * 6)
            for n in range(4):
                act.wait_ge(wa_in[n], 16)
                for k in range(KC):
                    act.activation(w_hi[:, n, k, :], stage_a[:, n, k, :], ACT.Copy,
                                   scale=g1c[:, k:k + 1] if n < 3 else 1.0).then_inc(w_hi_ok, 1)
            copy_T(0, xT_hi, XT, pe_xT, xT_hi_ok)
            load_columns(((b2c[:, :], ln2_b), (bff[:, :], b1)), vec2_in)
            act.dma_start(b2_row[:, :], b2.partition_broadcast(P)).then_inc(vec2_in, 16)
            act.wait_ge(wb_in, 16)
            for k in range(KC):
                act.activation(w1_hi[:, k, :], stage_b[:, k, :], ACT.Copy, scale=g2c[:, k:k + 1]).then_inc(w1_hi_ok, 1)
            act.wait_ge(bias_ready, 2)
            body(0, False, True)
            act.wait_ge(ff_bias_ready, 1)
            with act.Fori(1, NG - 1) as i:
                body(i, True, True)
            body(NG - 1, True, False)
            for half in range(2):
                copy_T(NG - 1, x2T_hi, TA, pe_x2T, x2T_hi_ok, half)
                gelus(NG - 1, half)

        @block.vector
        def _(dve):
            def stats(ln, i, j, src):
                dve.bn_stats(st[ln][:, j, :], src[:, j, :]).then_inc(stats_ok[ln], 1)
                hold_for(dve, stats_ok[ln], i * G + (j + 1), dve_passed)
                dve.bn_aggr(mv[ln][:, j, :], st[ln][:, j, :]).then_inc(mv_ok[ln], 1)

            def rsqrt_var(ln, i, part, half=None):
                step = [0 if part == 0 else 5 + 3 * (part - 1)]
                js = slice(graphs_of(half)[0], graphs_of(half)[-1] + 1)

                def link(ins):
                    step[0] += 1
                    ins.then_inc(rs_step[ln], 1)
                    wait(dve, rs_step[ln], done_before(i, RS_STEPS, half) + step[0])

                y, ve, nh, a, bits = (t[:, js] for t in (rstd[ln], *rs_tmp[ln], half_bits))
                if part == 0:
                    wait(dve, mv_ok[ln], i * G + js.stop)
                    dve.tensor_scalar(neg_mu[ln][:, js], mv[ln][:, js, 0], -1.0, None, ALU.mult).then_inc(rs_step[ln], 1)
                    step[0] += 1
                    link(dve.tensor_scalar(ve, mv[ln][:, js, 1], EPS, None, ALU.add))
                    link(dve.tensor_scalar(bits, ve.bitcast(I32), 1, None, ALU.logical_shift_right))
                    link(dve.tensor_scalar(y.bitcast(I32), bits, -1.0, RSQRT_GUESS, ALU.mult, ALU.add))
                    link(dve.tensor_scalar(nh, ve, -0.5, None, ALU.mult))
                else:
                    link(dve.tensor_tensor(a, y, y, ALU.mult))
                    link(dve.tensor_tensor(a, a, nh, ALU.mult))
                    link(dve.scalar_tensor_tensor(out=y, in0=a, scalar=1.5, in1=y, op0=ALU.add, op1=ALU.mult))

            def lo_T(i, lo, hi, bank, hi_ok, done, half=None):
                nodes = nodes_of(half)
                for c in range(KC):
                    wait(dve, hi_ok, done_before(i, KC, half) + (c + 1))
                    dve.tensor_tensor(lo[:, c, nodes], ps[:, bank + c, nodes], hi[:, c, nodes], ALU.subtract).then_inc(done, 1)

            def values(i):
                for j in (0, 1):
                    wait(dve, pe_v, i * G + (j + 1))
                    dve.tensor_copy(v_sb[:, j, :], ps[:, V_BANKS[j], 0:H]).then_inc(v_a_ok, 1)

            def maxima(i, j, chunks=range(KC)):
                if j == 0:
                    wait(dve, mask_ok, i + 1)
                if 0 in chunks:
                    hold_for(dve, pe_score, i * G + (j + 1), dve_passed)
                for c in chunks:
                    for r in range(R):
                        h = c * R + r
                        last = dve.tensor_tensor_reduce(masked[:, j % 2, h, :], ps[:, r, c * P:(c + 1) * P], mask[:, j, :],
                                                        1.0, -3.0e38, ALU.add, ALU.max, row_max[:, j % 2, h:h + 1])
                    last.then_inc(max_ok, 1)
                    wait(dve, max_ok, i * G * KC + (j * KC + c + 1))
                    dve.tensor_scalar(neg_max[:, j % 2, c * R:(c + 1) * R], row_max[:, j % 2, c * R:(c + 1) * R], -1.0, None,
                                      ALU.mult).then_inc(neg_max_ok, 1)

            def inverse(i, j, c):
                wait(dve, exp_ok, i * G * KC + (j * KC + c + 1))
                hs = slice(c * R, (c + 1) * R)
                dve.reciprocal(inv_sum[:, j % 2, hs], row_sum[:, j % 2, hs]).then_inc(inv_ok, 1)

            def probs_T(i, j):
                wait(dve, pe_pT, i * G * KC + (j * KC + KC))
                dve.tensor_copy(pT[:, R:2 * R, :], ps[:, TB, :].rearrange("p (h q) -> p h q", h=R)).then_inc(pT_b_ok, 1)

            def attn_lo(i, j):
                wait(dve, oT_hi_ok, i * G + (j + 1))
                dve.tensor_tensor(oT_lo[:, :, :], ps[:, TA, 0:KC * P].rearrange("p (c q) -> p c q", c=KC),
                                  oT_hi[:, :, :], ALU.subtract).then_inc(oT_lo_ok, 1)

            def residual(i, j):
                wait(dve, pe_wo, i * G + (j + 1))
                if j == 0:
                    wait(dve, x_res_ok, i * G + G)
                    wait(dve, x2_hat_a_ok, i * 2)
                    wait(dve, x2_res_ok, i * G)
                dve.tensor_tensor(x2[:, j, :], ps[:, WA, 0:H], x_res[:, j, :], ALU.add).then_inc(x2_ok, 1)
                wait(dve, x2_ok, i * G + (j + 1))
                stats(1, i, j, x2)

            def x2_hat_b(i):
                wait(dve, pe_x2T, i * KC)
                for j in (2, 3):
                    dve.tensor_scalar(x2_hat[:, j, :], x2[:, j, :], neg_mu[1][:, j:j + 1], rstd[1][:, j:j + 1],
                                      ALU.add, ALU.mult).then_inc(x2_hat_b_ok, 1)

            def gelu_lo(m, meanwhile=lambda f: None, half=None):
                nodes = nodes_of(half)
                for f in range(FC):
                    meanwhile(f)
                    wait(dve, h_hi_ok, done_before(m, FC, half) + (f + 1))
                    dve.tensor_tensor(h_lo[:, f, nodes], h_f32[:, f % 4, nodes], h_hi[:, f, nodes], ALU.subtract).then_inc(h_lo_ok, 1)

            def finish(m, j, bank=WB):
                wait(dve, pe_w2, m * G + (j + 1))
                wait(dve, x2_res_ok, m * G + (j + 1))
                wait(dve, y_stored, 1 + m * G * 16)
                dve.tensor_tensor(y_out[:, j, :], ps[:, bank, 0:H], x2_res[:, j, :], ALU.add).then_inc(y_ok, 1)

            def ln1_stats(i, j):
                if j == 0:
                    wait(dve, x_loaded, (i + 1) * 16)
                    wait(dve, x_hat_ok, i * G)
                stats(0, i, j, x_in)

            def split_mlp_weights(part):
                if part < KC:
                    dve.wait_ge(w1_hi_ok, part + 1)
                    dve.scalar_tensor_tensor(out=w1_lo[:, part, :], in0=stage_b[:, part, :], scalar=g2c[:, part:part + 1],
                                             in1=w1_hi[:, part, :], op0=ALU.mult, op1=ALU.subtract).then_inc(ff_lo_ok, 1)
                else:
                    half = slice((part - KC) * FC // 2, (part - KC + 1) * FC // 2)
                    dve.wait_ge(w2_hi_ok, FC // 2 * (part - KC + 1))
                    dve.tensor_tensor(w2_lo[:, half, :], stage_c[:, half, :], w2_hi[:, half, :],
                                      ALU.subtract).then_inc(ff_lo_ok, 1)

            def body(i, with_mlp, with_next):
                m = i - 1

                def meanwhile(f):
                    if with_next and 1 <= f <= RS_PARTS:
                        rsqrt_var(0, i + 1, f - 1)

                def end(j):
                    if with_mlp:
                        finish(m, j)

                if with_mlp:
                    residual(m, G - 1)
                    for part in range(RS_PARTS):
                        rsqrt_var(1, m, part)
                    x2_hat_b(m)
                values(i)
                maxima(i, 0)
                if with_mlp:
                    lo_T(m, x2T_lo, x2T_hi, TA, x2T_hi_ok, x2T_lo_ok)
                maxima(i, 1)
                for c in range(KC):
                    inverse(i, 0, c)
                if with_next:
                    for j in range(G):
                        ln1_stats(i + 1, j)
                if with_mlp:
                    gelu_lo(m, meanwhile)
                else:
                    for c in range(KC):
                        inverse(i, 1, c)
                    dve.wait_ge(ff_mm, 1)
                    dve.tensor_tensor(ff_bias[:, :], ps[:, WB, 0:FC], bff[:, :], ALU.add).then_inc(ff_bias_ready, 1)
                probs_T(i, 0)
                end(0)
                if with_mlp:
                    inverse(i, 1, 0)
                attn_lo(i, 0)
                if not with_mlp:
                    split_mlp_weights(0)
                    for f in range(FC):
                        meanwhile(f)
                maxima(i, 2, (0,))
                if with_mlp:
                    inverse(i, 1, 1)
                maxima(i, 2, (1,))
                end(1)
                probs_T(i, 1)
                inverse(i, 2, 0)
                inverse(i, 2, 1)
                residual(i, 0)
                attn_lo(i, 1)
                if not with_mlp:
                    split_mlp_weights(1)
                    split_mlp_weights(2)
                    split_mlp_weights(3)
                maxima(i, 3, (0,))
                probs_T(i, 2)
                maxima(i, 3, (1,))
                end(2)
                inverse(i, 3, 0)
                attn_lo(i, 2)
                residual(i, 1)
                inverse(i, 3, 1)
                if not with_next:
                    rsqrt_var(1, i, 0, 0)
                residual(i, 2)
                probs_T(i, 3)
                if not with_next:
                    rsqrt_var(1, i, 1, 0)
                else:
                    lo_T(i + 1, xT_lo, xT_hi, XT, xT_hi_ok, xT_lo_ok)
                end(3)
                if not with_next:
                    rsqrt_var(1, i, 2, 0)
                attn_lo(i, 3)
                if not with_next:
                    rsqrt_var(1, i, 3, 0)

            for j in range(G):
                ln1_stats(0, j)
            for part in range(RS_PARTS):
                rsqrt_var(0, 0, part)
            for j in (2, 3):
                dve.tensor_scalar(x_hat[:, j, :], x_in[:, j, :], neg_mu[0][:, j:j + 1], rstd[0][:, j:j + 1],
                                  ALU.add, ALU.mult).then_inc(x_hat_ok, 1)
            for n in range(4):
                for k in range(KC):
                    dve.wait_ge(w_hi_ok, n * KC + k + 1)
                    if n < 3:
                        ins = dve.scalar_tensor_tensor(out=w_lo[:, n, k, :], in0=stage_a[:, n, k, :], scalar=g1c[:, k:k + 1],
                                                       in1=w_hi[:, n, k, :], op0=ALU.mult, op1=ALU.subtract)
                    else:
                        ins = dve.tensor_tensor(w_lo[:, n, k, :], stage_a[:, n, k, :], w_hi[:, n, k, :], ALU.subtract)
                    ins.then_inc(w_lo_ok, 1)
            lo_T(0, xT_lo, xT_hi, XT, xT_hi_ok, xT_lo_ok)
            dve.wait_ge(bias_mm, 3)
            dve.tensor_tensor(qkv_bias[:, :, :], ps[:, TA, 0:3 * KC].rearrange("p (n c) -> p n c", n=3), bqkv[:, :, :],
                              ALU.add).then_inc(bias_ready, 1)
            dve.wait_ge(bias_ready, 1)
            dve.tensor_scalar(qkv_bias[:, 0, :], qkv_bias[:, 0, :], SCALE, None, ALU.mult).then_inc(bias_ready, 1)
            dve.tensor_copy(v_bias_wide[:, :, :], qkv_bias[:, 2, :].unsqueeze(2).broadcast_to([P, KC, P])).then_inc(wide_ready, 1)
            dve.wait_ge(orow_mm, 1)
            dve.wait_ge(bo_in, 16)
            dve.tensor_tensor(o_bias_row[:, :], ps[:, WB, 0:H], bo_row[:, :], ALU.add).then_inc(orow_ready, 1)
            body(0, False, True)
            with dve.Fori(1, NG - 1) as i:
                body(i, True, True)
            body(NG - 1, True, False)
            residual(NG - 1, G - 1)
            rsqrt_var(1, NG - 1, 0, 1)
            lo_T(NG - 1, x2T_lo, x2T_hi, TA, x2T_hi_ok, x2T_lo_ok, 0)
            for part in range(1, RS_PARTS):
                rsqrt_var(1, NG - 1, part, 1)
            x2_hat_b(NG - 1)
            gelu_lo(NG - 1, half=0)
            lo_T(NG - 1, x2T_lo, x2T_hi, TA, x2T_hi_ok, x2T_lo_ok, 1)
            finish(NG - 1, 0, LAST_BANKS[0])
            gelu_lo(NG - 1, half=1)
            for j in range(1, G):
                finish(NG - 1, j, LAST_BANKS[j])

        @block.gpsimd
        def _(pool):
            def hold(sem, value):
                hold_for(pool, sem, value, pool_passed)

            def make_mask(i):
                hold(adj_loaded, (i + 1) * 16)
                hold(max_ok, i * G * KC)
                nc.gpsimd.tensor_scalar(mask[:, :, :], adj_in[:, :, :], MASKED, -MASKED, ALU.mult, ALU.add).then_inc(mask_ok, 1)

            def apply_ln(ln, i, dst, src, graphs, done):
                hold(rs_step[ln], (i + 1) * RS_STEPS)
                for j in graphs:
                    nc.gpsimd.tensor_scalar(dst[:, j, :], src[:, j, :], neg_mu[ln][:, j:j + 1], rstd[ln][:, j:j + 1],
                                            ALU.add, ALU.mult).then_inc(done, 1)

            def ln1(i, graphs=range(G)):
                hold(pe_xT, i * KC)
                apply_ln(0, i, x_hat, x_in, graphs, x_hat_ok)

            def x2_hat_a(i):
                hold(pe_x2T, i * KC)
                apply_ln(1, i, x2_hat, x2, (0, 1), x2_hat_a_ok)

            def add_o_bias(i, j):
                wait(pool, x2_ok, i * G + (j - G + 1))
                nc.gpsimd.tensor_tensor(x_res[:, j, :], x_in[:, j, :], o_bias_row[:, :], ALU.add).then_inc(x_res_ok, 1)

            def normalise(i, j):
                for c in range(KC):
                    wait(pool, inv_ok, i * G * KC + (j * KC + c + 1))
                    hs = slice(c * R, (c + 1) * R)
                    nc.gpsimd.tensor_tensor(prob_n[:, j % 2, hs, :], prob[:, j % 2, hs, :],
                                            inv_sum[:, j % 2, hs].unsqueeze(2).broadcast_to([P, R, S]), ALU.mult).then_inc(prob_n_ok, 1)

            def add_b2(i, j):
                wait(pool, x2_ok, i * G + (j + 1))
                wait(pool, y_ok, 1 + i * G + (j - G + 1))
                nc.gpsimd.tensor_tensor(x2_res[:, j, :], x2[:, j, :], b2_row[:, :], ALU.add).then_inc(x2_res_ok, 1)

            def body(i, with_mlp, with_next):
                normalise(i, 0)
                if not with_mlp:
                    normalise(i, 1)
                if with_next:
                    ln1(i + 1)
                if with_mlp:
                    normalise(i, 1)
                normalise(i, 2)
                add_b2(i, 0)
                if with_next:
                    add_o_bias(i + 1, 0)
                normalise(i, 3)
                if with_next:
                    make_mask(i + 1)
                for j in range(1, G):
                    if j == G - 1 and not with_next:
                        x2_hat_a(i)
                    add_b2(i, j)
                    if with_next:
                        add_o_bias(i + 1, j)
                if with_next:
                    x2_hat_a(i)

            nc.gpsimd.memset(ident[:, :], 0.0).then_inc(ident_ready, 1)
            pool.wait_ge(ident_ready, 1)
            nc.gpsimd.affine_select(out=ident[:, :], in_=ident[:, :], compare_op=ALU.not_equal, fill=1.0, base=0,
                                    pattern=[[-1, P]], channel_multiplier=1).then_inc(ident_ready, 1)
            ln1(0, (0, 1))
            make_mask(0)
            pool.wait_ge(wc_in, 16)
            for f in range(FC):
                nc.gpsimd.tensor_copy(w2_hi[:, f, :], stage_c[:, f, :]).then_inc(w2_hi_ok, 1)
            pool.wait_ge(vec2_in, 16 * 3)
            pool.wait_ge(orow_ready, 1)
            for j in range(G):
                add_o_bias(0, j)
            body(0, False, True)
            with pool.Fori(1, NG - 1) as i:
                body(i, True, True)
            body(NG - 1, True, False)


_INS = ["x", "adj"] + ["L0_gnn_" + n for n in ("ln1_g", "ln1_b", "ln2_g", "ln2_b", "Wq", "bq", "Wk", "bk", "Wv", "bv",
                                               "Wo", "bo", "W1", "b1", "W2", "b2")]


def kernel(**inputs):
    import numpy as _np
    import concourse.bacc as _bacc
    from concourse import mybir as _mybir
    from concourse.bass_utils import run_bass_kernel_spmd as _run

    nc = _bacc.Bacc("TRN2", target_bir_lowering=False, num_devices=1)
    arrays, args = {}, []
    for name in _INS:
        a = _np.ascontiguousarray(inputs[name])
        arrays[f"in_{name}"] = a
        args.append(nc.dram_tensor(f"in_{name}", a.shape, _mybir.dt.from_np(a.dtype), kind="ExternalInput").ap())
    out = nc.dram_tensor("out_0", arrays["in_x"].shape, _mybir.dt.float32, kind="ExternalOutput").ap()
    graph_layer(nc, *args, out)
    r = _run(nc, [arrays], core_ids=[0])
    return r.results[0]["out_0"]
```
